# Optimizing a Trainium2 kernel written in Bass

```python
import numpy as np
import jax
import jax.numpy as jnp

def _softmax(x, axis=-1):
    return jax.nn.softmax(x, axis=axis)

def _gelu(x):
    return jax.nn.gelu(x, approximate=True)

def _silu(x):
    return jax.nn.silu(x)

def _sigmoid(x):
    return jax.nn.sigmoid(x)

def _layernorm(x, axis=-1, eps=1e-05):
    m = jnp.mean(x, axis=axis, keepdims=True)
    v = jnp.var(x, axis=axis, keepdims=True)
    return (x - m) / jnp.sqrt(v + eps)

def _scatter_add(tgt, idx, src, axis=0):
    return tgt.at[idx].add(src)

def _segment_sum(src, seg, n):
    return jax.ops.segment_sum(src, seg, n)
kernel_name = 'mk_adaln_d2_jaxref_r4_8c1d48'

def setup_inputs(seed: int=0):
    np.random.seed(seed)
    _w = jnp.asarray

    def _L0_attn_setup():
        import jax, jax.numpy as jnp
        import numpy as np
        N_HEAD = 16
        EPS = 1e-05
        ROPE_BASE = 10000.0
        key = jax.random.key(seed)
        ks = jax.random.split(key, 6)
        B, T, C = (2, 512, 256)
        s = 0.02
        return {'x': jax.random.normal(ks[0], (B, T, C), dtype=jnp.float32), 'wq': jax.random.normal(ks[1], (C, C), dtype=jnp.float32) * s, 'wk': jax.random.normal(ks[2], (C, C), dtype=jnp.float32) * s, 'wv': jax.random.normal(ks[3], (C, C), dtype=jnp.float32) * s, 'wproj': jax.random.normal(ks[4], (C, C), dtype=jnp.float32) * s, 'g_rms': jnp.ones((C // N_HEAD,), dtype=jnp.float32)}
    _L0_attn_in = _L0_attn_setup()

    def _L0_ffn_setup():
        import jax, jax.numpy as jnp
        import numpy as np
        D_IN, D_HID = (256, 1024)

        def _ternary(key, shape):
            return jax.random.randint(key, shape, -1, 2).astype(jnp.float32)

        def _tlin(x, w, s):
            return jnp.einsum('bsi,oi->bso', x, w) * s
        key = jax.random.key(seed)
        ks = jax.random.split(key, 12)
        inv = lambda fan: 1.0 / np.sqrt(fan).astype(np.float32)
        return {'x': jax.random.normal(ks[0], (4, 512, D_IN), dtype=jnp.float32), 'w1_w': _ternary(ks[1], (D_HID, D_IN)), 'w1_s': jax.random.uniform(ks[2], (D_HID,), dtype=jnp.float32) * inv(D_IN), 'w2_w': _ternary(ks[3], (D_HID, D_IN)), 'w2_s': jax.random.uniform(ks[4], (D_HID,), dtype=jnp.float32) * inv(D_IN), 'h1_w': _ternary(ks[5], (D_HID, D_HID)), 'h1_s': jax.random.uniform(ks[6], (D_HID,), dtype=jnp.float32) * inv(D_HID), 'h2_w': _ternary(ks[7], (D_HID, D_HID)), 'h2_s': jax.random.uniform(ks[8], (D_HID,), dtype=jnp.float32) * inv(D_HID), 'w3_w': _ternary(ks[9], (D_IN, D_HID)), 'w3_s': jax.random.uniform(ks[10], (D_IN,), dtype=jnp.float32) * inv(D_HID)}
    _L0_ffn_in = _L0_ffn_setup()
    _L0_c = _w((lambda *s: np.random.randn(*s).astype(np.float32) * 0.05)(8, 256))
    _L0_wmod = _w((lambda *s: np.random.randn(*s).astype(np.float32) * 0.05)(256, 6 * 256) * 256 ** (-0.5))

    def _L1_attn_setup():
        import jax, jax.numpy as jnp
        import numpy as np
        import math
        B, T, D, H = (4, 512, 256, 16)
        HD = D // H
        key = jax.random.key(seed)
        ks = jax.random.split(key, 10)
        s = 0.02
        return {'hidden_states': jax.random.normal(ks[0], (B, T, D), jnp.float32), 'Wq': jax.random.normal(ks[1], (H, D, HD), jnp.float32) * s, 'bq': jnp.zeros((H, HD), jnp.float32), 'Wk': jax.random.normal(ks[2], (H, D, HD), jnp.float32) * s, 'bk': jnp.zeros((H, HD), jnp.float32), 'Wv': jax.random.normal(ks[3], (H, D, HD), jnp.float32) * s, 'bv': jnp.zeros((H, HD), jnp.float32), 'Wo': jax.random.normal(ks[4], (H, HD, D), jnp.float32) * s, 'bo': jnp.zeros((H, D), jnp.float32), 'gate': jnp.ones((H,), jnp.float32)}
    _L1_attn_in = _L1_attn_setup()

    def _L1_ffn_setup():
        import jax, jax.numpy as jnp
        import numpy as np
        MICRO_BATCHES = 2
        TOP_K = 2
        LN_EPS = 1e-05
        B, S, D = (4, 1024, 256)
        E = 8
        DFF = 4 * D

        def _layernorm(x, g, b):
            mu = jnp.mean(x, axis=-1, keepdims=True)
            var = jnp.mean(jnp.square(x - mu), axis=-1, keepdims=True)
            return (x - mu) * jax.lax.rsqrt(var + LN_EPS) * g + b
        key = jax.random.key(seed)
        ks = jax.random.split(key, 12)
        sd = 1.0 / np.sqrt(D)
        sf = 1.0 / np.sqrt(DFF)
        return {'x': jax.random.normal(ks[0], (B, S, D), dtype=jnp.float32), 'ln_g': jnp.ones((D,), jnp.float32), 'ln_b': jnp.zeros((D,), jnp.float32), 'attn_w': jax.random.normal(ks[1], (D, D), jnp.float32) * sd, 'attn_b': jnp.zeros((D,), jnp.float32), 'gate_w': jax.random.normal(ks[2], (D, E), jnp.float32) * sd, 'w1': jax.random.normal(ks[3], (E, D, DFF), jnp.float32) * sd, 'b1': jnp.zeros((E, DFF), jnp.float32), 'w2': jax.random.normal(ks[4], (E, DFF, D), jnp.float32) * sf, 'b2': jnp.zeros((E, D), jnp.float32), 'next_w': jax.random.normal(ks[5], (D, D), jnp.float32) * sd, 'next_b': jnp.zeros((D,), jnp.float32)}
    _L1_ffn_in = _L1_ffn_setup()
    _L1_c = _w((lambda *s: np.random.randn(*s).astype(np.float32) * 0.05)(8, 256))
    _L1_wmod = _w((lambda *s: np.random.randn(*s).astype(np.float32) * 0.05)(256, 6 * 256) * 256 ** (-0.5))
    _d = {'L0_attn_x': _L0_attn_in['x'], 'L0_attn_wq': _L0_attn_in['wq'], 'L0_attn_wk': _L0_attn_in['wk'], 'L0_attn_wv': _L0_attn_in['wv'], 'L0_attn_wproj': _L0_attn_in['wproj'], 'L0_attn_g_rms': _L0_attn_in['g_rms'], 'L0_ffn_w1_w': _L0_ffn_in['w1_w'], 'L0_ffn_w1_s': _L0_ffn_in['w1_s'], 'L0_ffn_w2_w': _L0_ffn_in['w2_w'], 'L0_ffn_w2_s': _L0_ffn_in['w2_s'], 'L0_ffn_h1_w': _L0_ffn_in['h1_w'], 'L0_ffn_h1_s': _L0_ffn_in['h1_s'], 'L0_ffn_h2_w': _L0_ffn_in['h2_w'], 'L0_ffn_h2_s': _L0_ffn_in['h2_s'], 'L0_ffn_w3_w': _L0_ffn_in['w3_w'], 'L0_ffn_w3_s': _L0_ffn_in['w3_s'], 'L0_c': _L0_c, 'L0_wmod': _L0_wmod, 'L1_attn_Wq': _L1_attn_in['Wq'], 'L1_attn_bq': _L1_attn_in['bq'], 'L1_attn_Wk': _L1_attn_in['Wk'], 'L1_attn_bk': _L1_attn_in['bk'], 'L1_attn_Wv': _L1_attn_in['Wv'], 'L1_attn_bv': _L1_attn_in['bv'], 'L1_attn_Wo': _L1_attn_in['Wo'], 'L1_attn_bo': _L1_attn_in['bo'], 'L1_attn_gate': _L1_attn_in['gate'], 'L1_ffn_ln_g': _L1_ffn_in['ln_g'], 'L1_ffn_ln_b': _L1_ffn_in['ln_b'], 'L1_ffn_attn_w': _L1_ffn_in['attn_w'], 'L1_ffn_attn_b': _L1_ffn_in['attn_b'], 'L1_ffn_gate_w': _L1_ffn_in['gate_w'], 'L1_ffn_w1': _L1_ffn_in['w1'], 'L1_ffn_b1': _L1_ffn_in['b1'], 'L1_ffn_w2': _L1_ffn_in['w2'], 'L1_ffn_b2': _L1_ffn_in['b2'], 'L1_ffn_next_w': _L1_ffn_in['next_w'], 'L1_ffn_next_b': _L1_ffn_in['next_b'], 'L1_c': _L1_c, 'L1_wmod': _L1_wmod}
    _x0 = _d['L0_attn_x']
    _d['L0_attn_x'] = jax.random.normal(jax.random.fold_in(jax.random.key(seed), 1), (8, 512, 256), dtype=_x0.dtype)
    del _x0
    return _d

def reference(L0_attn_x, L0_attn_wq, L0_attn_wk, L0_attn_wv, L0_attn_wproj, L0_attn_g_rms, L0_ffn_w1_w, L0_ffn_w1_s, L0_ffn_w2_w, L0_ffn_w2_s, L0_ffn_h1_w, L0_ffn_h1_s, L0_ffn_h2_w, L0_ffn_h2_s, L0_ffn_w3_w, L0_ffn_w3_s, L0_c, L0_wmod, L1_attn_Wq, L1_attn_bq, L1_attn_Wk, L1_attn_bk, L1_attn_Wv, L1_attn_bv, L1_attn_Wo, L1_attn_bo, L1_attn_gate, L1_ffn_ln_g, L1_ffn_ln_b, L1_ffn_attn_w, L1_ffn_attn_b, L1_ffn_gate_w, L1_ffn_w1, L1_ffn_b1, L1_ffn_w2, L1_ffn_b2, L1_ffn_next_w, L1_ffn_next_b, L1_c, L1_wmod):

    def _L0_attn_ref(x, wq, wk, wv, wproj, g_rms):
        import jax, jax.numpy as jnp
        import numpy as np
        N_HEAD = 16
        EPS = 1e-05
        ROPE_BASE = 10000.0
        B, T, C = x.shape
        H = N_HEAD
        hd = C // H
        q = (x @ wq.T).reshape(B, T, H, hd)
        k = (x @ wk.T).reshape(B, T, H, hd)
        v = (x @ wv.T).reshape(B, T, H, hd)

        def rms(t):
            var = jnp.mean(t * t, axis=-1, keepdims=True) + EPS
            return g_rms * (t * jax.lax.rsqrt(var))
        q, k = (rms(q), rms(k))
        inv_freq = 1.0 / ROPE_BASE ** (jnp.arange(0, hd, 2, dtype=jnp.float32) / hd)
        freqs = jnp.outer(jnp.arange(T, dtype=jnp.float32), inv_freq)
        cos = jnp.cos(freqs).astype(jnp.bfloat16).astype(jnp.float32)[None, :, None, :]
        sin = jnp.sin(freqs).astype(jnp.bfloat16).astype(jnp.float32)[None, :, None, :]

        def rope(u):
            d = hd // 2
            u1, u2 = (u[..., :d], u[..., d:])
            return jnp.concatenate([u1 * cos + u2 * sin, -u1 * sin + u2 * cos], axis=-1)
        q, k = (rope(q), rope(k))
        qh = q.transpose(0, 2, 1, 3)
        kh = k.transpose(0, 2, 1, 3)
        vh = v.transpose(0, 2, 1, 3)
        scale = 1.0 / jnp.sqrt(jnp.float32(hd))
        scores = jnp.einsum('bhtd,bhsd->bhts', qh, kh) * scale + 1.0
        attn = jax.nn.softmax(scores, axis=-1)
        y = jnp.einsum('bhts,bhsd->bhtd', attn, vh)
        y = y.transpose(0, 2, 1, 3).reshape(B, T, C)
        return y @ wproj.T

    def _L0_ffn_ref(x, w1_w, w1_s, w2_w, w2_s, h1_w, h1_s, h2_w, h2_s, w3_w, w3_s):
        import jax, jax.numpy as jnp
        import numpy as np
        D_IN, D_HID = (256, 1024)

        def _ternary(key, shape):
            return jax.random.randint(key, shape, -1, 2).astype(jnp.float32)

        def _tlin(x, w, s):
            return jnp.einsum('bsi,oi->bso', x, w) * s
        h = jax.nn.silu(_tlin(x, w1_w, w1_s)) * _tlin(x, w2_w, w2_s)
        h = jax.nn.gelu(_tlin(h, h1_w, h1_s), approximate=False)
        h = jax.nn.gelu(_tlin(h, h2_w, h2_s), approximate=False)
        return _tlin(h, w3_w, w3_s)

    def _L1_attn_ref(hidden_states, Wq, bq, Wk, bk, Wv, bv, Wo, bo, gate):
        import jax, jax.numpy as jnp
        import numpy as np
        import math
        B, T, D, H = (4, 512, 256, 16)
        HD = D // H
        scale = 1.0 / math.sqrt(HD)
        q = jnp.einsum('btd,hdk->bhtk', hidden_states, Wq) + bq[None, :, None, :]
        k = jnp.einsum('btd,hdk->bhtk', hidden_states, Wk) + bk[None, :, None, :]
        v = jnp.einsum('btd,hdk->bhtk', hidden_states, Wv) + bv[None, :, None, :]
        scores = jnp.einsum('bhtk,bhsk->bhts', q, k) * scale
        weights = jax.nn.softmax(scores, axis=-1)
        out = jnp.einsum('bhts,bhsk->bhtk', weights, v)
        norms = jnp.linalg.norm(out, axis=-1)
        denom = jnp.maximum(norms.mean(axis=(0, 2)), 1e-05)
        out_norm = out / denom[None, :, None, None]
        gate_val = jnp.clip(gate, 0.0, 1.0)
        proj = (jnp.einsum('bhtk,hkd->bhtd', out_norm, Wo) + bo[None, :, None, :]) * gate_val[None, :, None, None]
        return proj.sum(axis=1) / H

    def _L1_ffn_ref(x, ln_g, ln_b, attn_w, attn_b, gate_w, w1, b1, w2, b2, next_w, next_b):
        import jax, jax.numpy as jnp
        import numpy as np
        MICRO_BATCHES = 2
        TOP_K = 2
        LN_EPS = 1e-05
        B, S, D = (4, 1024, 256)
        E = 8
        DFF = 4 * D

        def _layernorm(x, g, b):
            mu = jnp.mean(x, axis=-1, keepdims=True)
            var = jnp.mean(jnp.square(x - mu), axis=-1, keepdims=True)
            return (x - mu) * jax.lax.rsqrt(var + LN_EPS) * g + b
        Bx, Sx, Dx = x.shape
        N = Bx * Sx
        x_flat = x.reshape(N, Dx)
        x_attn = _layernorm(x_flat, ln_g, ln_b) @ attn_w + attn_b + x_flat
        logits = x_attn @ gate_w
        _ = jax.lax.top_k(logits, TOP_K)
        tpe = N // (MICRO_BATCHES * E)
        g = x_attn.reshape(MICRO_BATCHES, E, tpe, Dx)
        h = jax.nn.gelu(jnp.einsum('metd,edf->metf', g, w1) + b1[None, :, None, :], approximate=False)
        y = jnp.einsum('metf,efd->metd', h, w2) + b2[None, :, None, :]
        out = jax.nn.gelu(y @ next_w + next_b, approximate=False)
        return out.reshape(Bx, Sx, Dx)
    x = L0_attn_x
    mod = (_silu(L0_c) @ L0_wmod).reshape(L0_c.shape[0], 6, 1, -1)
    sa, ca, ga, sb, cb, gb = (mod[:, 0], mod[:, 1], mod[:, 2], mod[:, 3], mod[:, 4], mod[:, 5])
    ga = (2 * (ga >= 0) - 1) * jnp.maximum(jnp.abs(ga), 0.25)
    gb = (2 * (gb >= 0) - 1) * jnp.maximum(jnp.abs(gb), 0.25)
    h = _layernorm(x, axis=-1) * (1 + ca) + sa
    x = x + ga * _L0_attn_ref(h, L0_attn_wq, L0_attn_wk, L0_attn_wv, L0_attn_wproj, L0_attn_g_rms)
    h = _layernorm(x, axis=-1) * (1 + cb) + sb
    x = x + gb * _L0_ffn_ref(h, L0_ffn_w1_w, L0_ffn_w1_s, L0_ffn_w2_w, L0_ffn_w2_s, L0_ffn_h1_w, L0_ffn_h1_s, L0_ffn_h2_w, L0_ffn_h2_s, L0_ffn_w3_w, L0_ffn_w3_s)
    mod = (_silu(L1_c) @ L1_wmod).reshape(L1_c.shape[0], 6, 1, -1)
    sa, ca, ga, sb, cb, gb = (mod[:, 0], mod[:, 1], mod[:, 2], mod[:, 3], mod[:, 4], mod[:, 5])
    ga = (2 * (ga >= 0) - 1) * jnp.maximum(jnp.abs(ga), 0.25)
    gb = (2 * (gb >= 0) - 1) * jnp.maximum(jnp.abs(gb), 0.25)
    h = _layernorm(x, axis=-1) * (1 + ca) + sa
    x = x + ga * _L1_attn_ref(h, L1_attn_Wq, L1_attn_bq, L1_attn_Wk, L1_attn_bk, L1_attn_Wv, L1_attn_bv, L1_attn_Wo, L1_attn_bo, L1_attn_gate)
    h = _layernorm(x, axis=-1) * (1 + cb) + sb
    x = x + gb * _L1_ffn_ref(h, L1_ffn_ln_g, L1_ffn_ln_b, L1_ffn_attn_w, L1_ffn_attn_b, L1_ffn_gate_w, L1_ffn_w1, L1_ffn_b1, L1_ffn_w2, L1_ffn_b2, L1_ffn_next_w, L1_ffn_next_b)
    return x

_drawn_inputs = setup_inputs


def setup_inputs(seed=0):
    import zlib

    import numpy as np

    out = dict(_drawn_inputs(seed))
    spreads = {'L0_attn_g_rms': (1.0, 0.2),
     'L1_attn_bq': (0.0, 0.1),
     'L1_attn_bk': (0.0, 0.1),
     'L1_attn_bv': (0.0, 0.1),
     'L1_attn_bo': (0.0, 0.1),
     'L1_attn_gate': (1.0, 0.2),
     'L1_ffn_ln_g': (1.0, 0.2),
     'L1_ffn_ln_b': (0.0, 0.1),
     'L1_ffn_attn_b': (0.0, 0.1),
     'L1_ffn_b1': (0.0, 0.1),
     'L1_ffn_b2': (0.0, 0.1),
     'L1_ffn_next_b': (0.0, 0.1)}
    factors = {}
    for name, (base, spread) in spreads.items():
        noise = np.random.default_rng([zlib.crc32(name.encode()), seed]).standard_normal(out[name].shape)
        drawn = base * np.exp(spread * noise) if base else spread * noise
        out[name] = jnp.asarray(drawn.astype(out[name].dtype))
    for name, factor in factors.items():
        out[name] = (out[name] * factor).astype(out[name].dtype)
    return out
```

```python
import math
from contextlib import ExitStack

import concourse.bass as bass
import numpy as np
from concourse import mybir

F32 = mybir.dt.float32
F16 = mybir.dt.float16
ACT = mybir.ActivationFunctionType
ALU = mybir.AluOpType
AX = mybir.AxisListType.X

B, T, C, H, HD = 8, 512, 256, 16, 16
TT = T // 128
FT = C // 128
HG = 4
NG = H // HG
EPS = 1e-5
WS = 64.0
QROWS = 3 * HD + 1
BLK = 64
NEWTON = 3

MAX_SPLITS = [[3, 4, 2, 2, 3, 2, 0, 0], [4, 3, 3, 2, 2, 2, 0, 0]]


def mlp_slots():
    return {0: "O0p", 2: "O1p", 4: "TA0n", 6: "TA1n", 12: "TB0n", 14: "TB1n"}


def slots(layer):
    s = {3: "Y3p", 4: "YT1p", 5: "T0n", 6: "T1n", 7: "R1",
         8: "QK0n", 10: "QK1n", 11: "Y0", 12: "QK2n", 14: "QK3n", 15: "R2",
         16: "V0n", 17: "V1n", 19: "Y1", 20: "YT0", 21: "K0n", 22: "Qa0n", 23: "R3",
         24: "K1n", 25: "Qa1n", 26: "K2n", 27: "Y2", 28: "Qa2n", 29: "K3n", 30: "Qa3n", 31: "R0n"}
    if layer == 0:
        s |= {9: "P0p", 13: "P1p"}
    return dict(sorted(s.items()))


def kept(name, att, prev, nxt):
    return prev if name[-1] == "p" else nxt if name[-1] == "n" else att


class Batch:

    def __init__(self, table, b, i=None, par=None):
        self.b = b
        static = i is None
        self.att = not static or 0 <= b < B
        self.prev = not static or b >= 1
        self.nxt = not static or b < B - 1
        self.par = b % 2 if static else par
        self.pn = 1 - self.par
        self.hp = (b - 1) // 2 if static else i
        self.first = static and b == 0
        self.static = static
        self.slot = {s: n for s, n in table.items() if kept(n, self.att, self.prev, self.nxt)}
        self.order = {n: k for k, n in enumerate(self.slot.values())}
        every = list(table.values())
        n_of = lambda *f: sum(kept(n, *f) for n in every)
        before0 = n_of(False, False, True)
        before1 = before0 + n_of(True, False, True)
        full, last = len(every), n_of(True, True, False)
        if static and b <= 0:
            self.base = before0 * (b + 1)
        elif static and b == B:
            self.base = before1 + full * (B - 2) + last
        else:
            self.base = before1 + full * (b - 1)

    def job(self, name):
        return self.base + (self.order[name] + 1)

    def before(self, name):
        return self.base + self.order[name]

    def late(self, s):
        return self.slot.get(s - 1)


def run_batches(eng, table, body):
    for b in (-1, 0):
        body(Batch(table, b))
    with eng.Fori(0, (B - 2) // 2) as i:
        body(Batch(table, i * 2 + 1, i, 1))
        body(Batch(table, i * 2 + 2, i, 0))
    for b in (B - 1, B):
        body(Batch(table, b))


def phase_semaphores(nc, ctx, prefix):
    taken = []

    def cleared():
        nc.clear_and_free_semaphores(taken)
        nc.all_engine_barrier()

    def sem(name):
        taken.append(nc.alloc_semaphore(name=prefix + name))
        return taken[-1]

    ctx.callback(cleared)
    return sem


def attention(nc, layer, d, keep):
    L0 = layer == 0
    table = slots(layer)
    MAX_SPLIT = MAX_SPLITS[layer]
    MAX_AT = [sum(MAX_SPLIT[:u]) for u in range(8)]
    with ExitStack() as ctx:
        pre = f"A{layer}_"
        sb = lambda n, s, t=F32: ctx.enter_context(nc.sbuf_tensor(pre + n, s, t))
        pb = lambda n, s, t=F32: ctx.enter_context(nc.psum_tensor(pre + n, s, t))
        sem = phase_semaphores(nc, ctx, pre)

        xt = [sb(f"xt{k}", [128, TT, C]) for k in range(2)]
        xT = [sb(f"xT{k}", [128, FT, T]) for k in range(2)] if L0 else None
        cur = sb("cur", [128, 12])
        gcur = sb("gcur", [128, 12])
        st6 = sb("st6", [128, TT, 6])
        mv = sb("mv", [128, TT, 2])
        fence = sb("fence", [128, 1])
        ve = sb("ve", [128, TT])
        lnr = sb("lnr", [128, 3, TT])
        rstd = sb("rstd", [128, TT])
        xn = sb("xn", [128, TT, C])
        hf = sb("hf", [128, FT, T])
        hh = sb("hh", [128, FT, T], F16)
        hl = sb("hl", [128, FT, T], F16)
        w_st = sb("w_st", [128, FT, 3 * C])
        wh = sb("wh", [128, FT, 3 * C], F16)
        wl = sb("wl", [128, FT, 3 * C], F16)
        wp_h = sb("wp_h", [128, FT, C], F16) if L0 else None
        wp_l = sb("wp_l", [128, FT, C], F16) if L0 else None
        wp_st = sb("wp_st", [128, FT, C]) if L0 else None
        bqkv = None if L0 else sb("bqkv", [128, 3 * C])
        rope = sb("rope", [128, TT, 2, HD]) if L0 else None
        g16 = sb("g16", [128, HD]) if L0 else None
        qraw = sb("qraw", [128, 2, 2 * C]) if L0 else None
        sq = sb("sq", [128, 2 * C]) if L0 else None
        rv = sb("rv", [128, 2, 2 * H]) if L0 else None
        rln = sb("rln", [128, 2, 3, 2 * H]) if L0 else None
        rr = sb("rr", [128, 2 * H]) if L0 else None
        un = sb("un", [128, 2, 2 * C]) if L0 else None
        ro = sb("ro", [128, 2, 2 * C]) if L0 else None
        qo = sb("qo", [128, 2, 2 * C])
        Qs = [sb(f"Qs{k}", [128, TT, H, BLK], F16) for k in range(2)]
        Ks = sb("Ks", [128, TT, H, BLK], F16)
        KT = [sb(f"KT{k}", [128, H // 2, T], F16) for k in range(2)]
        QaT = [sb(f"QaT{k}", [128, H // 2, T], F16) for k in range(2)]
        QT = [sb(f"QT{k}", [128, 2, T], F16) for k in range(2)]
        V = [sb(f"V{k}", [128, TT, H, 32]) for k in range(2)]
        P = [sb(f"P{k}", [128, HG, 2, T]) for k in range(2)]
        ysb = sb("ysb", [128, T])
        rden = sb("rden", [128, 16])
        yn = sb("yn", [128, TT, C])
        yTh = sb("yTh", [128, FT, T], F16) if L0 else None
        yTl = sb("yTl", [128, FT, T], F16) if L0 else None
        yT = None if L0 else sb("yT", [128, FT, T])
        ysq = None if L0 else sb("ysq", [128, C])

        ST = pb("ST", [128, 2, 2, T])
        SM = pb("SM", [128, 2, T])
        AV = pb("AV", [128, T])
        X = pb("X", [128, T])
        X16 = X[:, :].bitcast(F16)

        w_ld, w_split, wp_ld, wp_split = sem("w_ld"), sem("w_split"), sem("wp_ld"), sem("wp_split")
        w_high = sem("w_high")
        tab_ld, tab = sem("tab_ld"), sem("tab")
        stack_init = sem("stack_init")
        xt_ld = [sem(f"xt_ld{k}") for k in range(2)]
        xT_ld = [sem(f"xT_ld{k}") for k in range(2)]
        x_st = [sem(f"x_st{k}") for k in range(2)]
        bns, agg, ve_s, ln_s, guess, newton, xn_s = (sem(n) for n in ("bns", "agg", "ve", "ln", "guess", "newton", "xn"))
        cur_s, gcur_s = sem("cur"), sem("gcur")
        h_high, h_low = sem("h_high"), sem("h_low")
        q_raw, q_sum, q_var, q_ln, q_guess, q_newton = (sem(n) for n in ("q_raw", "q_sum", "q_var", "q_ln", "q_guess", "q_newton"))
        q_scaled = sem("q_scaled")
        q_rot, qk_high, qk_low = sem("q_rot"), sem("qk_high"), sem("qk_low")
        job_done, job_out = sem("job_done"), sem("job_out")
        st_done, exp_done, max_mm, max_done, av_done, y_copied = (sem(n) for n in ("st", "exp", "max_mm", "max", "av", "y_copied"))
        y_rec, yT_high, y_sq, y_norm = sem("y_rec"), sem("yT_high"), sem("y_sq"), sem("y_norm")

        block = ctx.enter_context(nc.Block())

        def one(b, n=1):
            return bass.ds(b, n)

        @block.sync
        def _(sp):
            sp.dma_start(w_st[:, :, :], d["wqkv"].rearrange("(k p) n -> p k n", p=128)).then_inc(w_ld, 16)
            if L0:
                sp.dma_start(wp_st[:, :, :], d["wproj"].rearrange("(k p) n -> p k n", p=128)).then_inc(wp_ld, 16)
                sp.dma_start(rope[:, :, :, :], d["rope"].rearrange("(t p) a d -> p t a d", p=128)).then_inc(tab_ld, 16)
                sp.wait_ge(tab_ld, 16)
                sp.dma_start(g16[:, :], d["g_rms"].partition_broadcast(128)).then_inc(tab_ld, 16)
            else:
                sp.dma_start(bqkv[:, :], d["bqkv"].partition_broadcast(128)).then_inc(tab_ld, 16)

            def body(k):
                b = k.b
                if k.nxt:
                    if k.prev:
                        sp.wait_ge(xn_s, TT * b)
                    sp.dma_start(xt[k.pn][:, :, :],
                                 d["x_tok"][one(b + 1), :, :].rearrange("o (t p) c -> p (o t) c", p=128)
                                 ).then_inc(xt_ld[k.pn], 16)
                    if L0 and not k.prev:
                        sp.dma_start(xT[k.pn][:, :, :],
                                     d["x_feat"][one(b + 1), :, :].rearrange("o (f p) t -> p (o f) t", p=128)
                                     ).then_inc(xT_ld[k.pn], 16)
                if k.prev:
                    if L0:
                        sp.wait_ge(job_out, k.job("P1p"))
                        src = xT[k.pn]
                    else:
                        sp.wait_ge(job_out, k.job("YT1p"))
                        src = yT
                    sp.dma_start(d["x_out"][one(b - 1), :, :].rearrange("o (f p) t -> p (o f) t", p=128),
                                 src[:, :, :]).then_inc(x_st[k.pn], 16)
                    if L0 and k.nxt:
                        sp.wait_ge(x_st[k.pn], 16 * (k.hp + 1))
                        sp.dma_start(xT[k.pn][:, :, :],
                                     d["x_feat"][one(b + 1), :, :].rearrange("o (f p) t -> p (o f) t", p=128)
                                     ).then_inc(xT_ld[k.pn], 16)

            run_batches(sp, table, body)
            sp.wait_ge(x_st[0], 16 * B // 2)
            sp.wait_ge(x_st[1], 16 * B // 2)

        @block.gpsimd
        def _(pool):
            for k in range(2):
                nc.gpsimd.memset(Qs[k][:, :, :, :], 0.0).then_inc(stack_init, 1)
                nc.gpsimd.memset(V[k][:, :, :, HD:32], 1.0).then_inc(stack_init, 1)
            nc.gpsimd.memset(Ks[:, :, :, QROWS:BLK], 0.0).then_inc(stack_init, 1)
            nc.gpsimd.memset(Ks[:, :, :, QROWS - 1:QROWS], 1.0).then_inc(stack_init, 1)

            def body(k):
                if not k.nxt:
                    return
                n = k.b + 1
                for f in range(FT):
                    pool.wait_ge(job_out, k.job(f"T{f}n"))
                    nc.gpsimd.tensor_tensor(hl[:, f, :], hf[:, f, :], hh[:, f, :], ALU.subtract).then_inc(h_low, 1)
                for tt in range(TT):
                    if L0:
                        r = TT * n + tt
                        u3 = lambda a: a.rearrange("p (h d) -> p h d", d=HD)
                        tab3 = lambda a: a.unsqueeze(1).to_broadcast([128, 2 * H, a.shape[-1]])
                        pool.wait_ge(q_scaled, r + 1)
                        if not (k.static and k.b < 0 and tt == 0):
                            pool.wait_ge(q_rot, 4 * r)
                        if k.static and k.b < 0 and tt == 0:
                            pool.wait_ge(tab, 2)
                        nc.gpsimd.tensor_tensor(u3(ro[:, 0, :]), u3(un[:, tt % 2, :]), tab3(rope[:, tt, 0, :]),
                                                ALU.mult).then_inc(q_rot, 1)
                        hd2 = HD // 2
                        nc.gpsimd.tensor_tensor(u3(ro[:, 1, :])[:, :, 0:hd2], u3(un[:, tt % 2, :])[:, :, hd2:HD],
                                                tab3(rope[:, tt, 1, 0:hd2]), ALU.mult).then_inc(q_rot, 1)
                        nc.gpsimd.tensor_tensor(u3(ro[:, 1, :])[:, :, hd2:HD], u3(un[:, tt % 2, :])[:, :, 0:hd2],
                                                tab3(rope[:, tt, 1, hd2:HD]), ALU.mult).then_inc(q_rot, 1)
                        pool.wait_ge(q_rot, 4 * r + 3)
                        nc.gpsimd.tensor_tensor(qo[:, tt % 2, :], ro[:, 0, :], ro[:, 1, :],
                                                ALU.add).then_inc(q_rot, 1)
                    r = TT * n + tt
                    pool.wait_ge(qk_high, 2 * (r + 1))
                    q3 = qo[:, tt % 2, 0:C].rearrange("p (h d) -> p h d", d=HD)
                    k3 = qo[:, tt % 2, C:2 * C].rearrange("p (h d) -> p h d", d=HD)
                    nc.gpsimd.tensor_tensor(Qs[k.pn][:, tt, :, HD:2 * HD], q3, Qs[k.pn][:, tt, :, 0:HD],
                                            ALU.subtract).then_inc(qk_low, 1)
                    nc.gpsimd.tensor_tensor(Ks[:, tt, :, 2 * HD:3 * HD], k3, Ks[:, tt, :, 0:HD],
                                            ALU.subtract).then_inc(qk_low, 1)

            run_batches(pool, table, body)

        @block.scalar
        def _(act):
            nc.scalar.preload_act_table_set("natural_log_exp_and_others")
            act.wait_ge(w_ld, 16)
            nc.scalar.activation(wh[:, :, :], w_st[:, :, :], ACT.Copy, scale=WS).then_inc(w_high, 1)
            if L0:
                act.wait_ge(wp_ld, 16)
                nc.scalar.activation(wp_h[:, :, :], wp_st[:, :, :], ACT.Copy, scale=WS).then_inc(w_high, 1)

            def rsqrt_guess(v, ln, out, ready, count, ln_sem, out_sem, nth):
                act.wait_ge(ready, count)
                nc.scalar.activation(ln, v, ACT.Ln).then_inc(ln_sem, 1)
                act.wait_ge(ln_sem, nth)
                nc.scalar.activation(out, ln, ACT.Exp, scale=-0.5).then_inc(out_sem, 1)

            def out_of_bank(k, name):
                b = k.b
                if name in ("T0n", "T1n"):
                    f = int(name[1])
                    if f == 0:
                        act.wait_ge(cur_s, b + 2)
                    act.wait_ge(job_done, k.job(name))
                    if not (k.static and b < 0):
                        act.wait_ge(h_low, b * FT + (f + 1))
                    sc, bi = cur[:, 2 + f:3 + f], cur[:, 0 + f:1 + f]
                    nc.scalar.activation(hf[:, f, :], X[:, :], ACT.Identity, bias=bi, scale=sc).then_inc(h_high, 1)
                    nc.scalar.activation(hh[:, f, :], X[:, :], ACT.Identity, bias=bi, scale=sc).then_inc(job_out, 1)
                elif name[:2] == "QK" and L0:
                    tt = int(name[2])
                    r = (b + 1) * TT + tt
                    if not (k.static and b < 0 and tt == 0):
                        act.wait_ge(q_sum, r)
                    if not (k.static and b < 0 and tt < 2):
                        act.wait_ge(q_scaled, r - 1)
                    act.wait_ge(job_done, k.job(name))
                    nc.scalar.activation(qraw[:, tt % 2, :], X[:, :], ACT.Copy, scale=1 / WS).then_inc(q_raw, 1)
                    nc.scalar.activation(sq[:, :], X[:, :], ACT.Square, scale=1 / WS).then_inc(job_out, 1)
                elif name[0] == "V" and L0:
                    v = int(name[1])
                    act.wait_ge(job_done, k.job(name))
                    nc.scalar.activation(V[k.pn][:, 2 * v:2 * v + 2, :, 0:HD],
                                         X[:, :].rearrange("p (t h d) -> p t h d", t=2, d=HD),
                                         ACT.Copy, scale=1 / WS).then_inc(job_out, 1)
                elif name[0] == "K":
                    j = int(name[1])
                    act.wait_ge(job_done, k.job(name))
                    nc.scalar.activation(KT[k.pn][:, 2 * j:2 * j + 2, :],
                                         X16.rearrange("p (a t) -> p a t", a=2), ACT.Copy).then_inc(job_out, 1)
                elif name[:2] == "YT":
                    f = int(name[2])
                    act.wait_ge(job_done, k.job(name))
                    if L0:
                        nc.scalar.activation(yTh[:, f, :], X[:, :], ACT.Copy).then_inc(yT_high, 1)
                    else:
                        if f == 0 and k.prev and not k.first:
                            act.wait_ge(x_st[k.pn], 16 * (k.hp + 1))
                        nc.scalar.activation(yT[:, f, :], X[:, :], ACT.Copy).then_inc(job_out, 1)
                elif name[0] == "Y" and not L0:
                    g0 = int(name[1])
                    m = (b - 1 if name[-1] == "p" else b) * NG + g0
                    act.wait_ge(job_out, k.job(name))
                    if not (k.first and g0 == 0):
                        act.wait_ge(y_norm, m)
                    nc.scalar.activation(ysq[:, :].rearrange("p (t c) -> p t c", t=TT),
                                         yn[:, :, g0 * 64:g0 * 64 + 64], ACT.Square).then_inc(y_sq, 1)

            def stack(k, tt):
                b = k.b
                r = (b + 1) * TT + tt
                if L0:
                    act.wait_ge(q_rot, r * 4 + 4)
                else:
                    act.wait_ge(job_out, k.job(f"QK{tt}n"))
                if k.static and b < 0 and tt == 0:
                    act.wait_ge(stack_init, 6)
                dup = lambda a: a.rearrange("p (h d) -> p h d", d=HD).unsqueeze(2).to_broadcast(
                    [128, H, 2, HD])
                nc.scalar.activation(
                    Qs[k.pn][:, tt, :, :].rearrange("p h (a d) -> p h a d", d=HD)[:, :, 0:3:2, :],
                    dup(qo[:, tt % 2, 0:C]), ACT.Copy).then_inc(qk_high, 1)
                nc.scalar.activation(
                    Ks[:, tt, :, 0:2 * HD].rearrange("p h (a d) -> p h a d", d=HD),
                    dup(qo[:, tt % 2, C:2 * C]), ACT.Copy).then_inc(qk_high, 1)

            def body(k):
                b = k.b
                for s in range(32):
                    g, u = s // 8, s % 8
                    G = b * NG + g
                    tt = (s - (14 if L0 else 10)) // 2
                    if k.nxt and s % 2 == 0 and 0 <= tt < TT:
                        stack(k, tt)
                    if s in k.slot:
                        out_of_bank(k, k.slot[s])
                    if u == 2 and (k.att or (k.prev and g == 0)) and not (k.first and g == 0):
                        act.wait_ge(av_done, G * 2)
                        nc.scalar.activation(ysb[:, :], AV[:, :], ACT.Copy).then_inc(y_copied, 1)
                    if k.att:
                        head, half = u % 4, u // 4
                        act.wait_ge(st_done, G * 8 + (u + 1))
                        if not (k.first and g == 0):
                            act.wait_ge(av_done, G * 2 + (half - 1))
                        nc.scalar.activation(P[half][:, head, :, :], ST[:, u % 2, :, :], ACT.Exp,
                                             scale=1.0 / math.sqrt(HD)).then_inc(exp_done, 1)
                    if k.nxt and s == 1:
                        rsqrt_guess(ve[:, :], lnr[:, 0, :], lnr[:, 1, :], ve_s, b + 2, ln_s, guess, b + 2)
                    for tt in range(TT):
                        if k.nxt and L0 and s == 8 + 2 * tt + 2:
                            nth = (b + 1) * TT + (tt + 1)
                            rsqrt_guess(rv[:, tt % 2, :], rln[:, tt % 2, 0, :], rln[:, tt % 2, 1, :], q_var, nth, q_ln, q_guess, nth)

            run_batches(act, table, body)

        @block.vector
        def _(dve):
            dve.wait_ge(w_high, 1)
            nc.vector.scalar_tensor_tensor(out=wl[:, :, :], in0=w_st[:, :, :], scalar=WS, in1=wh[:, :, :],
                                           op0=ALU.mult, op1=ALU.subtract).then_inc(w_split, 1)
            if L0:
                dve.wait_ge(w_high, 2)
                nc.vector.scalar_tensor_tensor(out=wp_l[:, :, :], in0=wp_st[:, :, :], scalar=WS, in1=wp_h[:, :, :],
                                               op0=ALU.mult, op1=ALU.subtract).then_inc(w_split, 1)
                dve.wait_ge(tab_ld, 32)
                gb = lambda a: a.unsqueeze(1).to_broadcast([128, TT, a.shape[-1]])
                hd2 = HD // 2
                nc.vector.tensor_tensor(rope[:, :, 0, :], rope[:, :, 0, :], gb(g16[:, :]), ALU.mult).then_inc(tab, 1)
                nc.vector.tensor_tensor(rope[:, :, 1, 0:hd2], rope[:, :, 1, 0:hd2], gb(g16[:, hd2:HD]), ALU.mult)
                nc.vector.tensor_tensor(rope[:, :, 1, hd2:HD], rope[:, :, 1, hd2:HD], gb(g16[:, 0:hd2]),
                                        ALU.mult).then_inc(tab, 1)
            else:
                dve.wait_ge(tab_ld, 16)

            def refine(v, guess_, work, out, ready, nth, chain):
                dve.wait_ge(ready, nth)
                nc.vector.tensor_tensor(work, guess_, guess_, ALU.mult).then_inc(chain, 1)
                dve.wait_ge(chain, nth * NEWTON - 2)
                nc.vector.scalar_tensor_tensor(out=work, in0=work, scalar=-0.5, in1=v,
                                               op0=ALU.mult, op1=ALU.mult).then_inc(chain, 1)
                dve.wait_ge(chain, nth * NEWTON - 1)
                nc.vector.scalar_tensor_tensor(out=out, in0=work, scalar=1.5, in1=guess_,
                                               op0=ALU.add, op1=ALU.mult).then_inc(chain, 1)

            def out_of_bank(k, name):
                b = k.b
                if name[0] == "R":
                    g2 = int(name[1])
                    dve.wait_ge(job_done, k.job(name))
                    nc.vector.tensor_copy(QT[g2 % 2][:, :, :],
                                          X16.rearrange("p (a t) -> p a t", a=2)).then_inc(job_out, 1)
                elif name[:2] == "Qa":
                    j = int(name[2])
                    dve.wait_ge(job_done, k.job(name))
                    nc.vector.tensor_copy(QaT[k.pn][:, 2 * j:2 * j + 2, :],
                                          X16.rearrange("p (a t) -> p a t", a=2)).then_inc(job_out, 1)
                elif name[:2] == "QK" and not L0:
                    tt = int(name[2])
                    dve.wait_ge(job_done, k.job(name))
                    r = (b + 1) * TT + tt
                    if not (k.static and b < 0 and tt < 2):
                        dve.wait_ge(qk_low, (r - 1) * 2)
                    nc.vector.scalar_tensor_tensor(out=qo[:, tt % 2, :], in0=X[:, :], scalar=1 / WS,
                                                   in1=bqkv[:, 0:2 * C], op0=ALU.mult, op1=ALU.add).then_inc(job_out, 1)
                elif name[0] == "V" and not L0:
                    v = int(name[1])
                    dve.wait_ge(job_done, k.job(name))
                    if k.static and b < 0:
                        dve.wait_ge(stack_init, 6)
                    for h in range(2):
                        ins = nc.vector.scalar_tensor_tensor(
                            out=V[k.pn][:, 2 * v + h, :, 0:HD],
                            in0=X[:, h * C:h * C + C].rearrange("p (h d) -> p h d", d=HD), scalar=1 / WS,
                            in1=bqkv[:, 2 * C:3 * C].rearrange("p (h d) -> p h d", d=HD), op0=ALU.mult, op1=ALU.add)
                    ins.then_inc(job_out, 1)
                elif name[:2] == "YT" and L0:
                    f = int(name[2])
                    m = ((b - 1) if name[-1] == "p" else b) * FT + (f + 1)
                    dve.wait_ge(yT_high, m)
                    nc.vector.tensor_tensor(yTl[:, f, :], X[:, :], yTh[:, f, :], ALU.subtract).then_inc(job_out, 1)
                elif name[0] == "Y" and name[1] != "T":
                    g0 = int(name[1])
                    m = ((b - 1) if name[-1] == "p" else b) * NG + g0
                    dve.wait_ge(job_done, k.job(name))
                    y4 = X[:, :].rearrange("p (t j c) -> p t j c", t=TT, j=HG)
                    nc.vector.reciprocal(rden[:, :].rearrange("p (t j) -> p t j", t=TT),
                                         y4[:, :, :, HD]).then_inc(y_rec, 1)
                    dve.wait_ge(y_rec, m + 1)
                    nc.vector.tensor_tensor(
                        yn[:, :, g0 * 64:g0 * 64 + 64].rearrange("p t (j d) -> p t j d", j=HG), y4[:, :, :, 0:HD],
                        rden[:, :].rearrange("p (t j) -> p t j", t=TT).unsqueeze(3).to_broadcast([128, TT, HG, HD]),
                        ALU.mult).then_inc(job_out, 1)
                elif name[0] == "P":
                    f = int(name[1])
                    if f == 0:
                        dve.wait_ge(gcur_s, b)
                        dve.wait_ge(xT_ld[k.pn], 16 * (k.hp + 1))
                    dve.wait_ge(job_done, k.job(name))
                    nc.vector.scalar_tensor_tensor(out=xT[k.pn][:, f, :], in0=X[:, :], scalar=gcur[:, 4 + f:5 + f],
                                                   in1=xT[k.pn][:, f, :], op0=ALU.mult, op1=ALU.add).then_inc(job_out, 1)

            def body(k):
                b = k.b
                n = b + 1
                for s in range(32):
                    g, u = s // 8, s % 8
                    G1 = n * NG if g == NG - 1 else b * NG + (g + 1)
                    name = k.slot.get(s, "")
                    if name[:1] == "R" and not (k.static and b < 0 or k.first and g == 0):
                        dve.wait_ge(st_done, (b * NG + g) * 8)
                    if name:
                        out_of_bank(k, name)
                    if (k.att and g < NG - 1) or (k.nxt and g == NG - 1):
                        par = k.pn if g == NG - 1 else k.par
                        for t in range(MAX_AT[u], MAX_AT[u] + MAX_SPLIT[u]):
                            j, tt = t // TT, t % TT
                            head = ((g + 1) % NG) * HG + j
                            dve.wait_ge(max_mm, G1 * 16 + (t + 1))
                            nc.vector.tensor_reduce(Qs[par][:, tt, head, QROWS - 1:QROWS], SM[:, t % 2, :], AX,
                                                    ALU.max, negate=True).then_inc(max_done, 1)
                    if k.nxt:
                        if s == 0:
                            dve.wait_ge(xt_ld[k.pn], 16 * (k.hp + 2) if not (k.static and b < 0) else 16)
                            for tt in range(TT):
                                nc.vector.bn_stats(st6[:, tt, :], xt[k.pn][:, tt, :]).then_inc(bns, 1)
                            dve.wait_ge(bns, n * TT + TT)
                            nc.vector.memset(fence[:, :], 0.0)
                            for tt in range(TT):
                                nc.vector.bn_aggr(mv[:, tt, :], st6[:, tt, :]).then_inc(agg, 1)
                            dve.wait_ge(agg, n * TT + TT)
                            nc.vector.tensor_scalar(ve[:, :], mv[:, :, 1], EPS, None, ALU.add).then_inc(ve_s, 1)
                        if s == 2:
                            refine(ve[:, :], lnr[:, 1, :], lnr[:, 2, :], rstd[:, :], guess, n + 1, newton)
                            dve.wait_ge(newton, (n + 1) * NEWTON)
                            for tt in range(TT):
                                nc.vector.tensor_scalar(xn[:, tt, :], xt[k.pn][:, tt, :], mv[:, tt, 0:1],
                                                        rstd[:, tt:tt + 1], ALU.subtract, ALU.mult).then_inc(xn_s, 1)
                            nc.vector.tensor_copy(cur[:, :], keep["mod"][:, layer, one(n), :].rearrange("p o c -> p (o c)")
                                                  ).then_inc(cur_s, 1)
                        for tt in range(TT):
                            nth = n * TT + (tt + 1)
                            if L0 and s == 8 + 2 * tt + 1:
                                dve.wait_ge(job_out, k.job(f"QK{tt}n"))
                                nc.vector.tensor_reduce(rv[:, tt % 2, :], sq[:, :].rearrange("p (h d) -> p h d", d=HD), AX,
                                                        ALU.add).then_inc(q_sum, 1)
                                dve.wait_ge(q_sum, nth)
                                nc.vector.tensor_scalar(rv[:, tt % 2, :], rv[:, tt % 2, :], 1.0 / HD, EPS, ALU.mult,
                                                        ALU.add).then_inc(q_var, 1)
                            if L0 and s == 8 + 2 * tt + 3:
                                if not (k.static and b < 0 and tt == 0):
                                    dve.wait_ge(q_scaled, nth - 1)
                                refine(rv[:, tt % 2, :], rln[:, tt % 2, 1, :], rln[:, tt % 2, 2, :],
                                       rr[:, :], q_guess, nth, q_newton)
                                dve.wait_ge(q_newton, nth * NEWTON)
                                if not (k.static and b < 0 and tt < 2):
                                    dve.wait_ge(q_rot, (nth - 3) * 4 + 3)
                                nc.vector.tensor_tensor(un[:, tt % 2, :].rearrange("p (h d) -> p h d", d=HD),
                                                        qraw[:, tt % 2, :].rearrange("p (h d) -> p h d", d=HD),
                                                        rr[:, :].unsqueeze(2).to_broadcast([128, 2 * H, HD]),
                                                        ALU.mult).then_inc(q_scaled, 1)
                    if L0 and k.prev and s == 8:
                        nc.vector.tensor_copy(gcur[:, :], keep["mod"][:, layer, one(b - 1), :].rearrange("p o c -> p (o c)")
                                              ).then_inc(gcur_s, 1)
                    if not L0:
                        for g0, at in ((3, 5), (0, 13), (1, 21), (2, 29)):
                            if s == at and (k.prev if g0 == 3 else k.att):
                                m = ((b - 1) if g0 == 3 else b) * NG + g0
                                bb = (b - 1) if g0 == 3 else b
                                dve.wait_ge(y_sq, m + 1)
                                nc.vector.tensor_reduce(
                                    keep["norm2"][:, one(bb * NG + g0), :],
                                    ysq[:, :].rearrange("p (o t d) -> p o t d", o=1, d=HD), AX,
                                    ALU.add).then_inc(y_norm, 1)

            run_batches(dve, table, body)

        @block.tensor
        def _(pe):
            id32, id16 = keep["id32"], keep["id16"]
            pe.wait_ge(w_split, 2 if L0 else 1)

            def product(out, pairs):
                todo = [(a, c) for ah, al, ch, cl in pairs for a, c in ((ah, ch), (ah, cl), (al, ch))]
                for n_, (a, c) in enumerate(todo):
                    ins = nc.tensor.matmul(out, a, c, start=n_ == 0, stop=n_ == len(todo) - 1)
                return ins

            def body(k):
                b = k.b
                n = b + 1

                def job(name):
                    if not (k.static and k.before(name) == 0):
                        pe.wait_ge(job_out, k.before(name))
                    kind = name.rstrip("pn")
                    if kind[0] == "T":
                        f = int(kind[1])
                        pe.wait_ge(xn_s, (n + 1) * TT)
                        for tt in range(TT):
                            ins = nc.tensor.transpose(X[:, tt * 128:tt * 128 + 128],
                                                      xn[:, tt, f * 128:f * 128 + 128], id32[:, :])
                    elif kind[:2] == "QK":
                        tt = int(kind[2])
                        if tt == 0:
                            pe.wait_ge(h_low, (n + 1) * FT)
                        t_ = slice(tt * 128, tt * 128 + 128)
                        ins = product(X[:, :], [(hh[:, f, t_], hl[:, f, t_], wh[:, f, 0:2 * C], wl[:, f, 0:2 * C])
                                                for f in range(FT)])
                    elif kind[0] == "V":
                        for h in range(2):
                            tt = 2 * int(kind[1]) + h
                            t_ = slice(tt * 128, tt * 128 + 128)
                            ins = product(X[:, h * C:h * C + C],
                                          [(hh[:, f, t_], hl[:, f, t_], wh[:, f, 2 * C:3 * C], wl[:, f, 2 * C:3 * C])
                                           for f in range(FT)])
                    elif kind[0] in "KQR":
                        src = Ks if kind[0] == "K" else Qs[k.par if (kind[0] == "R" and name[-1] != "n") else k.pn]
                        if kind == "K0":
                            pe.wait_ge(qk_low, (n + 1) * TT * 2)
                        if kind[0] == "R":
                            G1 = (n * NG if kind == "R0" else b * NG + int(kind[1]))
                            pe.wait_ge(max_done, (G1 + 1) * 16)
                        j = int(kind[-1])
                        for a in range(2):
                            pair = 2 * j + a
                            for tt in range(TT):
                                o = (a * TT + tt) * 128
                                ins = nc.tensor.transpose(
                                    X16[:, o:o + 128],
                                    src[:, tt, 2 * pair:2 * pair + 2, :].rearrange("p h c -> p (h c)"), id16[:, :])
                    elif kind[:2] == "YT":
                        f = int(kind[2])
                        for tt in range(TT):
                            ins = nc.tensor.transpose(X[:, tt * 128:tt * 128 + 128],
                                                      yn[:, tt, f * 128:f * 128 + 128], id32[:, :])
                    elif kind[0] == "Y":
                        g0 = int(kind[1])
                        pe.wait_ge(y_copied, ((b - 1) if g0 == 3 else b) * NG + (g0 + 1))
                        for tt in range(TT):
                            ins = nc.tensor.transpose(X[:, tt * 128:tt * 128 + 128],
                                                      ysb[:, tt * 128:tt * 128 + 128], id32[:, :])
                    elif kind[0] == "P":
                        f = int(kind[1])
                        f_ = slice(f * 128, f * 128 + 128)
                        ins = product(X[:, :], [(wp_h[:, c, f_], wp_l[:, c, f_], yTh[:, c, :], yTl[:, c, :])
                                                for c in range(FT)])
                    ins.then_inc(job_done, 1)

                def values(gg, half, par, count):
                    pe.wait_ge(exp_done, count * 8 + (4 * half + 4))
                    if half == 0 and not (k.first and gg == 0):
                        pe.wait_ge(y_copied, count)
                    for st in range(2):
                        for j in range(HG):
                            ins = nc.tensor.matmul(AV[32 * j:32 * j + 32, :], V[par][:, 2 * half + st, gg * HG + j, :],
                                                   P[half][:, j, st, :], start=half == 0 and st == 0,
                                                   stop=half == 1 and st == 1)
                    ins.then_inc(av_done, 1)

                def scores(g, u):
                    if u == 0:
                        pe.wait_ge(job_out, k.base if g == 0 else k.job(f"R{g}"))
                    if not (k.first and g == 0 and u < 2):
                        pe.wait_ge(exp_done, (b * NG + g) * 8 + (u - 1))
                    j, half = u % 4, u // 4
                    r = slice(BLK * (j % 2), BLK * (j % 2) + QROWS)
                    for st in range(2):
                        o = (2 * half + st) * 128
                        ins = nc.tensor.matmul(ST[:, u % 2, st, :], KT[k.par][r, 2 * g + j // 2, o:o + 128],
                                               QT[g % 2][r, j // 2, :], start=True, stop=True)
                    ins.then_inc(st_done, 1)

                def raw_scores(g, tiles):
                    wrap = g == NG - 1
                    if not (k.nxt if wrap else k.att):
                        return
                    par = k.pn if wrap else k.par
                    G1 = n * NG if wrap else b * NG + (g + 1)
                    for t in tiles:
                        j, tt = t // TT, t % TT
                        gg = (g + 1) % NG
                        if wrap and t == 0:
                            pe.wait_ge(job_out, k.job("Qa0n"))
                        if not (k.static and b < 0 and t < 2):
                            pe.wait_ge(max_done, G1 * 16 + (t - 1))
                        r = slice(BLK * (j % 2), BLK * (j % 2) + HD)
                        nc.tensor.matmul(SM[:, t % 2, :], QaT[par][r, 2 * gg + j // 2, tt * 128:tt * 128 + 128],
                                         KT[par][r, 2 * gg + j // 2, :], start=True, stop=True).then_inc(max_mm, 1)

                for s in range(32):
                    g, u = s // 8, s % 8
                    tiles = range(MAX_AT[u], MAX_AT[u] + MAX_SPLIT[u])
                    if s in k.slot:
                        job(k.slot[s])
                    if u == 0:
                        raw_scores(g, tiles[:2])
                    if k.att:
                        scores(g, u)
                    if u > 0:
                        raw_scores(g, tiles[:2])
                    if u == 1 and (k.att or (k.prev and g == 0)) and not (k.first and g == 0):
                        values((g - 1) % NG, 1, k.pn if g == 0 else k.par, b * NG + (g - 1))
                    if u == 5 and k.att:
                        values(g, 0, k.par, b * NG + g)
                    raw_scores(g, tiles[2:])

            run_batches(pe, table, body)


def setup(nc, d, keep):
    with ExitStack() as ctx:
        sb = lambda n, s, t=F32: ctx.enter_context(nc.sbuf_tensor("S_" + n, s, t))
        sem = phase_semaphores(nc, ctx, "S_")
        wm = sb("wm", [128, 2, FT, 6 * C])
        cc = sb("cc", [128, 2, FT, B])
        cs = sb("cs", [128, 2, FT, B])
        ones = sb("ones", [128, 128])
        mod = keep["mod"][:, :, :, :].rearrange("p l b (a f) -> p l b a f", f=FT)
        MP = ctx.enter_context(nc.psum_tensor("S_MP", [128, 2, 12, B], F32))
        wm_ld, c_ld = [sem("wm0"), sem("wm1")], sem("c_ld")
        ones_s, ident, silu, mm, moved, gated = (sem(n) for n in ("ones", "ident", "silu", "mm", "moved", "gated"))
        block = ctx.enter_context(nc.Block())

        @block.sync
        def _(sp):
            sp.dma_start(cc[:, :, :, :], d["c"].rearrange("l (k p) b -> p l k b", p=128)).then_inc(c_ld, 16)
            for l in range(2):
                sp.dma_start(wm[:, l, :, :], d["wmod"][l, :, :].rearrange("(k p) n -> p k n", p=128)
                             ).then_inc(wm_ld[l], 16)

        @block.gpsimd
        def _(pool):
            nc.gpsimd.memset(ones[:, :], 1.0).then_inc(ones_s, 1)
            pool.wait_ge(ones_s, 1)
            for t in (keep["id32"], keep["id16"]):
                nc.gpsimd.affine_select(out=t[:, :], in_=ones[:, :], pattern=[[-1, 128]], compare_op=ALU.is_equal,
                                        fill=0.0, base=0, channel_multiplier=1).then_inc(ident, 1)
            pool.wait_ge(ident, 2)

        @block.scalar
        def _(act):
            act.wait_ge(c_ld, 16)
            nc.scalar.activation(cs[:, :, :, :], cc[:, :, :, :], ACT.Silu).then_inc(silu, 1)

        @block.tensor
        def _(pe):
            pe.wait_ge(silu, 1)
            for l in range(2):
                pe.wait_ge(wm_ld[l], 16)
                for m in range(12):
                    for k in range(FT):
                        ins = nc.tensor.matmul(MP[:, l, m, :], wm[:, l, k, m * 128:m * 128 + 128], cs[:, l, k, :],
                                               start=k == 0, stop=k == FT - 1)
            ins.then_inc(mm, 1)

        @block.vector
        def _(dve):
            dve.wait_ge(mm, 1)
            for l in range(2):
                nc.vector.tensor_copy(mod[:, l, :, :, :].rearrange("p b a f -> p (a f) b"), MP[:, l, :, :]
                                      ).then_inc(moved, 1)
            dve.wait_ge(moved, 2)
            sgn = cc
            n = 0
            for l in range(2):
                for a in (1, 4):
                    nc.vector.tensor_scalar(mod[:, l, :, a, :], mod[:, l, :, a, :], 1.0, None, ALU.add
                                            ).then_inc(gated, 1)
                    n += 1
                for a in (2, 5):
                    sv = sgn[:, l, :, :].rearrange("p f b -> p b f")
                    dve.wait_ge(gated, n)
                    nc.vector.tensor_scalar(sv, mod[:, l, :, a, :], 0.0, 2.0, ALU.is_ge, ALU.mult).then_inc(gated, 1)
                    nc.vector.scalar_tensor_tensor(out=mod[:, l, :, a, :], in0=mod[:, l, :, a, :], scalar=-1.0,
                                                   in1=mod[:, l, :, a, :], op0=ALU.mult, op1=ALU.max).then_inc(gated, 1)
                    n += 2
                    dve.wait_ge(gated, n)
                    nc.vector.tensor_scalar(mod[:, l, :, a, :], mod[:, l, :, a, :], 0.25,
                                            1 / WS if (l, a) == (0, 2) else 1.0, ALU.max, ALU.mult).then_inc(gated, 1)
                    n += 1
                    dve.wait_ge(gated, n)
                    nc.vector.scalar_tensor_tensor(out=mod[:, l, :, a, :], in0=sv, scalar=-1.0,
                                                   in1=mod[:, l, :, a, :], op0=ALU.add, op1=ALU.mult).then_inc(gated, 1)
                    n += 1
            dve.wait_ge(gated, n)


HID = 4 * C
HM = HID // 128
HS = 64.0
BLOCKS = 3 * HM + FT


def mlp0(nc, d, keep):
    table = mlp_slots()
    with ExitStack() as ctx:
        sb = lambda n, s, t=F32: ctx.enter_context(nc.sbuf_tensor("B_" + n, s, t))
        pb = lambda n, s, t=F32: ctx.enter_context(nc.psum_tensor("B_" + n, s, t))
        sem = phase_semaphores(nc, ctx, "B_")

        xT = [sb(f"xT{k}", [128, FT, T]) for k in range(2)]
        xo = sb("xo", [128, FT, T])
        xtok, xn, otok = sb("xtok", [128, TT, C]), sb("xn", [128, TT, C]), sb("otok", [128, TT, C])
        cur, gcur = sb("cur", [128, 12]), sb("gcur", [128, 12])
        gs = sb("gs", [128, FT])
        st6, mv, fence = sb("st6", [128, TT, 6]), sb("mv", [128, TT, 2]), sb("fence", [128, 1])
        ve, lnr, rstd = sb("ve", [128, TT]), sb("lnr", [128, 3, TT]), sb("rstd", [128, TT])
        hf = sb("hf", [128, FT, T])
        hh = [sb(f"hh{k}", [128, FT, T], F16) for k in range(2)]
        hl = [sb(f"hl{k}", [128, FT, T], F16) for k in range(2)]
        CH = 2 * HID
        NW = (2 * FT * HID + 2 * HM * HID + HM * C) // CH
        w_st = sb("w_st", [128, 2, CH])
        wh, wl = sb("wh", [128, NW * CH], F16), sb("wl", [128, NW * CH], F16)
        off = {"w1": 0, "w2": FT * HID, "h1": 2 * FT * HID, "h2": (2 * FT + HM) * HID, "w3": (2 * FT + 2 * HM) * HID}
        sv = sb("sv", [128, 4, HM])
        s3 = sb("s3", [128, FT])
        lomax, flag, flag_i = sb("lomax", [128, NW + 1]), sb("flag", [128, 1]), sb("flag_i", [128, 1], mybir.dt.int32)
        af = sb("af", [128, 3, T])
        uf = sb("uf", [128, 2, T])
        Hh = [sb(f"Hh{k}", [128, HM, T], F16) for k in range(2)]
        Hl = [sb(f"Hl{k}", [128, HM, T], F16) for k in range(2)]
        PA, PD, X = pb("PA", [128, 4, T]), pb("PD", [128, 2, T]), pb("X", [128, T])

        w_ld = [sem(f"w_ld{k}") for k in range(2)]
        w_high, w_low, w_abs, s_ld, s_scaled = sem("w_high"), sem("w_low"), sem("w_abs"), sem("s_ld"), sem("s_scaled")
        all_max, flag_s, flag_is = sem("all_max"), sem("flag_s"), sem("flag_is")
        x_ld = [sem(f"x_ld{k}") for k in range(2)]
        xo_st, ot_st = sem("xo_st"), sem("ot_st")
        bns, agg, ve_s, ln_s, guess, newton, xn_s = (sem(n) for n in ("bns", "agg", "ve", "ln", "guess", "newton", "xn"))
        cur_s, gcur_s, gs_s, h_high, h_low = sem("cur"), sem("gcur"), sem("gs"), sem("h_high"), sem("h_low")
        job_done, job_out = sem("job_done"), sem("job_out")
        a_done, a_out, d_done, d_out = sem("a_done"), sem("a_out"), sem("d_done"), sem("d_out")
        high, split = sem("high"), sem("split")
        NA, ND = 3 * HM, HM + FT

        block = ctx.enter_context(nc.Block())

        def one(b):
            return bass.ds(b, 1)

        @block.sync
        def _(sp):
            for c in range(NW):
                if c >= 2:
                    sp.wait_ge(w_low, c - 1)
                sp.dma_start(w_st[:, c % 2, :], d["w_ffn0"][c, :, :]).then_inc(w_ld[c % 2], 16)
                if c == 0:
                    sp.dma_start(sv[:, :, :], d["s_ffn0"][:, 0:4 * HM].rearrange("p (a m) -> p a m", a=4)
                                 ).then_inc(s_ld, 16)
                    sp.wait_ge(s_ld, 16)
                    sp.dma_start(s3[:, :], d["s_ffn0"][:, 4 * HM:4 * HM + FT]).then_inc(s_ld, 16)

            def body(k):
                b = k.b
                if k.nxt:
                    if k.prev:
                        sp.wait_ge(d_out, ND * b)
                    sp.dma_start(xT[k.pn][:, :, :], d["x1"][one(b + 1), :, :].rearrange("o (f p) t -> p (o f) t", p=128)
                                 ).then_inc(x_ld[k.pn], 16)
                if k.prev:
                    if not k.nxt:
                        sp.wait_ge(d_out, ND * b)
                    sp.dma_start(d["x2"][one(b - 1), :, :].rearrange("o (f p) t -> p (o f) t", p=128), xo[:, :, :]
                                 ).then_inc(xo_st, 16)
                    sp.wait_ge(job_out, k.job("O1p"))
                    sp.dma_start(d["x2_tok"][one(b - 1), :, :].rearrange("o (t p) c -> p (o t) c", p=128), otok[:, :, :]
                                 ).then_inc(ot_st, 16)

            run_batches(sp, table, body)
            sp.wait_ge(xo_st, 16 * B)
            sp.wait_ge(ot_st, 16 * B)

        @block.gpsimd
        def _(pool):
            pool.wait_ge(w_abs, NW + 1)
            nc.gpsimd.partition_all_reduce(flag[:, :], lomax[:, NW:NW + 1], 128, bass.bass_isa.ReduceOp.max
                                           ).then_inc(all_max, 1)

            def body(k):
                if k.nxt:
                    for f in range(FT):
                        pool.wait_ge(job_out, k.job(f"TB{f}n"))
                        nc.gpsimd.tensor_tensor(hl[k.pn][:, f, :], hf[:, f, :], hh[k.pn][:, f, :], ALU.subtract
                                                ).then_inc(h_low, 1)

            run_batches(pool, table, body)

        @block.scalar
        def _(act):
            for c in range(NW):
                act.wait_ge(w_ld[c % 2], 16 * (c // 2 + 1))
                nc.scalar.activation(wh[:, c * CH:c * CH + CH], w_st[:, c % 2, :], ACT.Copy).then_inc(w_high, 1)

            def body(k):
                b = k.b
                for s in range(BLOCKS):
                    name = k.late(s)
                    if name is not None:
                        act.wait_ge(job_done, k.job(name))
                        i = int(name[-2])
                    if name in ("TA0n", "TA1n"):
                        nc.scalar.activation(xtok[:, 2 * i:2 * i + 2, :], X[:, :].rearrange("p (t c) -> p t c", t=2),
                                             ACT.Copy).then_inc(job_out, 1)
                    elif name in ("O0p", "O1p"):
                        nc.scalar.activation(otok[:, 2 * i:2 * i + 2, :], X[:, :].rearrange("p (t c) -> p t c", t=2),
                                             ACT.Copy).then_inc(job_out, 1)
                    elif name in ("TB0n", "TB1n"):
                        if i == 0:
                            act.wait_ge(cur_s, b + 2)
                        if not (k.static and b < 0):
                            act.wait_ge(h_low, b * FT + (i + 1))
                        sc, bi = cur[:, 8 + i:9 + i], cur[:, 6 + i:7 + i]
                        nc.scalar.activation(hf[:, i, :], X[:, :], ACT.Identity, bias=bi, scale=sc).then_inc(h_high, 1)
                        nc.scalar.activation(hh[k.pn][:, i, :], X[:, :], ACT.Identity, bias=bi, scale=sc
                                             ).then_inc(job_out, 1)
                    if k.nxt and s == 9:
                        act.wait_ge(ve_s, b + 2)
                        nc.scalar.activation(lnr[:, 0, :], ve[:, :], ACT.Ln).then_inc(ln_s, 1)
                        act.wait_ge(ln_s, b + 2)
                        nc.scalar.activation(lnr[:, 1, :], lnr[:, 0, :], ACT.Exp, scale=-0.5).then_inc(guess, 1)
                    if k.prev and s == 16:
                        act.wait_ge(ot_st, 16 * b)
                    if k.att and s < NA:
                        t = NA * b + s
                        act.wait_ge(a_done, t + 1)
                        if not (k.first and s < 3):
                            act.wait_ge(split, t - 2)
                        if k.first and s == 0:
                            act.wait_ge(s_scaled, 1)
                        which, m = (0, s) if s < HM else (2, s - HM) if s < 2 * HM else (3, s - 2 * HM)
                        nc.scalar.activation(af[:, s % 3, :], PA[:, s % 4, :], ACT.Silu if s < HM else ACT.Gelu,
                                             scale=sv[:, which, m:m + 1]).then_inc(a_out, 1)

            run_batches(act, table, body)

        @block.vector
        def _(dve):
            for c in range(NW):
                dve.wait_ge(w_high, c + 1)
                nc.vector.tensor_tensor(wl[:, c * CH:c * CH + CH], w_st[:, c % 2, :], wh[:, c * CH:c * CH + CH],
                                        ALU.subtract).then_inc(w_low, 1)
                dve.wait_ge(w_low, c + 1)
                nc.vector.tensor_reduce(lomax[:, c:c + 1], wl[:, c * CH:c * CH + CH], AX, ALU.max,
                                        apply_absolute_value=True).then_inc(w_abs, 1)
            dve.wait_ge(w_abs, NW)
            nc.vector.tensor_reduce(lomax[:, NW:NW + 1], lomax[:, 0:NW], AX, ALU.max).then_inc(w_abs, 1)
            dve.wait_ge(s_ld, 32)
            nc.vector.tensor_scalar(sv[:, 2:4, :], sv[:, 2:4, :], 1 / HS, None, ALU.mult).then_inc(s_scaled, 1)
            dve.wait_ge(all_max, 1)
            nc.vector.tensor_scalar(flag[:, :], flag[:, :], 0.0, None, ALU.is_gt).then_inc(flag_s, 1)
            dve.wait_ge(flag_s, 1)
            nc.vector.tensor_copy(flag_i[:, :], flag[:, :]).then_inc(flag_is, 1)

            def body(k):
                b = k.b
                n = b + 1
                for s in range(BLOCKS):
                    if k.nxt and s == 8:
                        dve.wait_ge(job_out, k.job("TA1n"))
                        for tt in range(TT):
                            nc.vector.bn_stats(st6[:, tt, :], xtok[:, tt, :]).then_inc(bns, 1)
                        dve.wait_ge(bns, n * TT + TT)
                        nc.vector.memset(fence[:, :], 0.0)
                        for tt in range(TT):
                            nc.vector.bn_aggr(mv[:, tt, :], st6[:, tt, :]).then_inc(agg, 1)
                        dve.wait_ge(agg, n * TT + TT)
                        nc.vector.tensor_scalar(ve[:, :], mv[:, :, 1], EPS, None, ALU.add).then_inc(ve_s, 1)
                        nc.vector.tensor_copy(cur[:, :], keep["mod"][:, 0, one(n), :].rearrange("p o c -> p (o c)")
                                              ).then_inc(cur_s, 1)
                    if k.nxt and s == 10:
                        dve.wait_ge(guess, n + 1)
                        nc.vector.tensor_tensor(lnr[:, 2, :], lnr[:, 1, :], lnr[:, 1, :], ALU.mult).then_inc(newton, 1)
                        dve.wait_ge(newton, (n + 1) * NEWTON - 2)
                        nc.vector.scalar_tensor_tensor(out=lnr[:, 2, :], in0=lnr[:, 2, :], scalar=-0.5, in1=ve[:, :],
                                                       op0=ALU.mult, op1=ALU.mult).then_inc(newton, 1)
                        dve.wait_ge(newton, (n + 1) * NEWTON - 1)
                        nc.vector.scalar_tensor_tensor(out=rstd[:, :], in0=lnr[:, 2, :], scalar=1.5, in1=lnr[:, 1, :],
                                                       op0=ALU.add, op1=ALU.mult).then_inc(newton, 1)
                        dve.wait_ge(newton, (n + 1) * NEWTON)
                        for tt in range(TT):
                            nc.vector.tensor_scalar(xn[:, tt, :], xtok[:, tt, :], mv[:, tt, 0:1], rstd[:, tt:tt + 1],
                                                    ALU.subtract, ALU.mult).then_inc(xn_s, 1)
                    if k.att and s == NA - 1:
                        nc.vector.tensor_copy(gcur[:, :], keep["mod"][:, 0, one(b), :].rearrange("p o c -> p (o c)")
                                              ).then_inc(gcur_s, 1)
                        dve.wait_ge(gcur_s, n)
                        nc.vector.scalar_tensor_tensor(out=gs[:, :], in0=gcur[:, 10:12], scalar=1 / HS, in1=s3[:, :],
                                                       op0=ALU.mult, op1=ALU.mult).then_inc(gs_s, 1)
                    if not k.att:
                        continue
                    if s < NA:
                        t = NA * b + s
                        dve.wait_ge(a_out, t + 1)
                        src = af[:, s % 3, :]
                        if s < HM:
                            dve.wait_ge(d_done, ND * b + (s + 1))
                            nc.vector.scalar_tensor_tensor(out=uf[:, s % 2, :], in0=PD[:, s % 2, :],
                                                           scalar=sv[:, 1, s:s + 1], in1=src,
                                                           op0=ALU.mult, op1=ALU.mult).then_inc(d_out, 1)
                            dve.wait_ge(d_out, ND * b + (s + 1))
                            src = uf[:, s % 2, :]
                        w, m = (s // HM) % 2, s % HM
                        nc.vector.tensor_scalar(Hh[w][:, m, :], src, HS, None, ALU.mult).then_inc(high, 1)
                        dve.wait_ge(high, t + 1)
                        nc.vector.scalar_tensor_tensor(out=Hl[w][:, m, :], in0=src, scalar=HS, in1=Hh[w][:, m, :],
                                                       op0=ALU.mult, op1=ALU.subtract).then_inc(split, 1)
                    else:
                        f = s - NA
                        if f == 0:
                            dve.wait_ge(gs_s, n)
                            if k.prev:
                                dve.wait_ge(xo_st, 16 * b)
                        dve.wait_ge(d_done, ND * b + (HM + f + 1))
                        nc.vector.scalar_tensor_tensor(out=xo[:, f, :], in0=PD[:, f % 2, :], scalar=gs[:, f:f + 1],
                                                       in1=xT[k.par][:, f, :], op0=ALU.mult, op1=ALU.add
                                                       ).then_inc(d_out, 1)

            run_batches(dve, table, body)

        @block.tensor
        def _(pe):
            id32 = keep["id32"]
            pe.wait_ge(w_low, NW)
            pe.wait_ge(flag_is, 1)
            inexact = pe.value_load(flag_i[0:1, 0:1], min_val=0, max_val=1)

            def w(name, cols, kt, m, low=False):
                o = off[name] + kt * cols + m * 128
                return (wl if low else wh)[:, o:o + 128]

            def gemm(out, name, cols, m, kts, xh, xl, lows, start, stop):
                for kt in kts:
                    ops = [(w(name, cols, kt, m), xh(kt)), (w(name, cols, kt, m), xl(kt))]
                    if lows:
                        ops.append((w(name, cols, kt, m, True), xh(kt)))
                    for n_, (a, c) in enumerate(ops):
                        ins = nc.tensor.matmul(out, a, c, start=start and kt == 0 and n_ == 0,
                                               stop=stop and kt == kts[-1] and n_ == len(ops) - 1)
                return ins

            def one_pass(k, lows):
                b = k.b
                n = b + 1

                def job(name):
                    if not (k.static and k.before(name) == 0):
                        pe.wait_ge(job_out, k.before(name))
                    i = int(name[-2])
                    if name[:2] == "TB":
                        pe.wait_ge(xn_s, (n + 1) * TT)
                        for tt in range(TT):
                            ins = nc.tensor.transpose(X[:, tt * 128:tt * 128 + 128], xn[:, tt, i * 128:i * 128 + 128],
                                                      id32[:, :])
                    else:
                        if name == "TA0n":
                            pe.wait_ge(x_ld[k.pn], 16 * (k.hp + 2))
                        if name == "O0p":
                            pe.wait_ge(d_out, ND * b)
                        src = xo if name[0] == "O" else xT[k.pn]
                        for a in range(2):
                            for f in range(FT):
                                o = (a * FT + f) * 128
                                tt = 2 * i + a
                                ins = nc.tensor.transpose(X[:, o:o + 128], src[:, f, tt * 128:tt * 128 + 128],
                                                          id32[:, :])
                    ins.then_inc(job_done, 1)

                for s in range(BLOCKS + 1):
                    if k.att and s < HM:
                        if s == 0:
                            pe.wait_ge(h_low, FT * n)
                        if not (k.first and s < 4):
                            pe.wait_ge(a_out, NA * b + (s - 3))
                        xh, xl = (lambda kt: hh[k.par][:, kt, :]), (lambda kt: hl[k.par][:, kt, :])
                        gemm(PA[:, s % 4, :], "w1", HID, s, range(FT), xh, xl, lows, True, True).then_inc(a_done, 1)
                        if not (k.first and s < 2):
                            pe.wait_ge(d_out, ND * b + (s - 1))
                        gemm(PD[:, s % 2, :], "w2", HID, s, range(FT), xh, xl, lows, True, True).then_inc(d_done, 1)
                    elif k.att:
                        def of(s_):
                            if s_ < NA:
                                return (PA[:, s_ % 4, :], "h1" if s_ < 2 * HM else "h2", HID, s_ % HM, s_ // HM - 1,
                                        a_done)
                            return PD[:, s_ % 2, :], "w3", C, s_ - NA, 2, d_done
                        if s < BLOCKS:
                            out, name, cols, m, lay, _d = of(s)
                            if m == 0:
                                pe.wait_ge(split, NA * b + (HM * lay + HM - 2))
                            if s < NA:
                                pe.wait_ge(a_out, NA * b + (s - 3))
                            else:
                                pe.wait_ge(d_out, ND * b + (HM + m - 1))
                            src = lay % 2
                            gemm(out, name, cols, m, range(HM - 2), lambda kt: Hh[src][:, kt, :],
                                 lambda kt: Hl[src][:, kt, :], lows, True, False)
                        last = s - 1 >= HM
                        same = s < BLOCKS and s % HM != 0
                        if last and (same or s == BLOCKS):
                            finish(k, of, s - 1, lows)
                        nxt_first = s % HM == HM - 1 and s < NA
                        if nxt_first:
                            finish(k, of, s, lows)
                    if s in k.slot:
                        job(k.slot[s])

            def finish(k, of, s_, lows):
                out, name, cols, m, lay, done = of(s_)
                if m == 0:
                    pe.wait_ge(split, NA * k.b + (HM * lay + HM))
                src = lay % 2
                gemm(out, name, cols, m, range(HM - 2, HM), lambda kt: Hh[src][:, kt, :],
                     lambda kt: Hl[src][:, kt, :], lows, False, True).then_inc(done, 1)

            def body(k):
                if not k.att:
                    one_pass(k, False)
                    return
                with pe.If(inexact > 0):
                    one_pass(k, True)
                with pe.Else():
                    one_pass(k, False)

            run_batches(pe, table, body)


E8 = 8
EH = T // 2


NORM_AT = (5, 11)


def moe_slots():
    return {1: "Z0n", 2: "Z1n", 4: "TA0n", 5: "TA1n", 8: "TB0n", 9: "TB1n", 10: "TC0n", 11: "TC1n",
            13: "TD0n", 14: "TD1n", 15: "G0n", 16: "G1n"}


def experts(nc, d, keep):
    table = moe_slots()
    NS = 18
    NA = HM + FT
    with ExitStack() as ctx:
        sb = lambda n, s, t=F32: ctx.enter_context(nc.sbuf_tensor("D_" + n, s, t))
        pb = lambda n, s, t=F32: ctx.enter_context(nc.psum_tensor("D_" + n, s, t))
        sem = phase_semaphores(nc, ctx, "D_")

        nsum, rinv = sb("nsum", [128, H]), sb("rinv", [128, H])
        hsel, gates, selw = sb("hsel", [128, FT, H]), sb("gates", [128, H]), sb("selw", [128, 2, FT, H])
        rsc, gsc = sb("rsc", [128, FT]), sb("gsc", [128, FT])
        ones = sb("ones", [128, 128])
        bo, gcol, bob = sb("bo", [H, C]), sb("gcol", [H, 1]), sb("bob", [128, FT])
        wsm = sb("wsm", [128, 3, FT, C])
        wsh, wsl = sb("wsh", [128, 3, FT, C], F16), sb("wsl", [128, 3, FT, C], F16)
        vec = sb("vec", [128, 4, FT])
        eb = sb("eb", [128, E8, HM + FT])
        w_st = sb("w_st", [128, 2, FT * HID])
        eh = [sb(f"eh{k}", [128, 2, FT * HID], F16) for k in range(2)]
        el = [sb(f"el{k}", [128, 2, FT * HID], F16) for k in range(2)]
        yT = [sb(f"yT{k}", [128, FT, 2, EH]) for k in range(2)]
        x3 = [sb(f"x3{k}", [128, FT, 2, EH]) for k in range(2)]
        yf, yh, yl = sb("yf", [128, FT, T]), sb("yh", [128, FT, T], F16), sb("yl", [128, FT, T], F16)
        cur, gcur = sb("cur", [128, 2, 12]), sb("gcur", [128, 2, 12])
        eb_cur = sb("eb_cur", [128, HM + FT])
        gab, ga64 = sb("gab", [128, 2, FT]), sb("ga64", [128, 2, FT])
        zf = sb("zf", [128, FT, T])
        xtok, xn = sb("xtok", [128, TT, C]), sb("xn", [128, TT, C])
        st6, mv, fence = sb("st6", [128, TT, 6]), sb("mv", [128, TT, 2]), sb("fence", [128, 1])
        ve, lnr, rstd = sb("ve", [128, TT]), sb("lnr", [128, 3, TT]), sb("rstd", [128, TT])
        hf = sb("hf", [128, FT, T])
        h2f, h2h, h2l = sb("h2f", [128, FT, T]), sb("h2h", [128, FT, T], F16), sb("h2l", [128, FT, T], F16)
        gf = sb("gf", [128, FT, T])
        gh = [sb(f"gh{k}", [128, FT, T], F16) for k in range(2)]
        gl = [sb(f"gl{k}", [128, FT, T], F16) for k in range(2)]
        af = sb("af", [128, 2, T])
        Hh, Hl = sb("Hh", [128, HM, T], F16), sb("Hl", [128, HM, T], F16)
        y2f, y2h, y2l = sb("y2f", [128, FT, T]), sb("y2h", [128, FT, T], F16), sb("y2l", [128, FT, T], F16)
        of, xo = sb("of", [128, FT, T]), sb("xo", [128, FT, 2, EH])

        PA, PW, X = pb("PA", [128, 4, T]), pb("PW", [128, 2, T]), pb("X", [128, T])

        c_ld = [sem(f"c_ld{k}") for k in range(8)]
        root, nred, ntot, ninv, nsel, gsel, bsum, bob_s = (sem(n) for n in ("root", "nred", "ntot", "ninv", "nsel",
                                                                           "gsel", "bsum", "bob_s"))
        cw_sc, cw_high, cw_low, ones_s = sem("cw_sc"), sem("cw_high"), sem("cw_low"), sem("ones_s")
        w_ld = [sem(f"w_ld{k}") for k in range(2)]
        y_ld = [sem(f"y_ld{k}") for k in range(2)]
        x_ld = [sem(f"x_ld{k}") for k in range(2)]
        e_high, e_low = sem("e_high"), sem("e_low")
        y_norm, y_low, cur_s, gcur_s, ebc, gab_s = (sem(n) for n in ("y_norm", "y_low", "cur", "gcur", "ebc", "gab"))
        x3_s, bns, agg, ve_s, ln_s, guess, newton, xn_s = (sem(n) for n in ("x3", "bns", "agg", "ve", "ln", "guess",
                                                                            "newton", "xn"))
        h2_high, h2_low, g_sum, g_high, g_low = (sem(n) for n in ("h2_high", "h2_low", "g_sum", "g_high", "g_low"))
        job_done, job_out = sem("job_done"), sem("job_out")
        a_done, a_out, high, split = sem("a_done"), sem("a_out"), sem("high"), sem("split")
        w2_done, y2_s, w2_out, y2_low, x4_s, o_st = (sem(n) for n in ("w2_done", "y2_s", "w2_out", "y2_low", "x4", "o_st"))

        block = ctx.enter_context(nc.Block())

        def one(b):
            return bass.ds(b, 1)

        def halves(t, q, par, f=None):
            rows = slice(0, C) if f is None else slice(f * 128, f * 128 + 128)
            a = t[:, one(q), rows, par * EH:par * EH + EH]
            return a

        @block.sync
        def _(sp):
            sp.dma_start(hsel[:, :, :], d["head_of"]).then_inc(c_ld[0], 16)
            sp.dma_start(gates[:, :], d["gate"].partition_broadcast(128)).then_inc(c_ld[1], 16)
            sp.dma_start(bo[:, :], d["bo"]).then_inc(c_ld[2], 16)
            sp.dma_start(gcol[:, :], d["gate"].unsqueeze(1)).then_inc(c_ld[3], 16)
            sp.dma_start(wsm[:, :, :, :], d["w_small"].rearrange("a (k p) n -> p a k n", p=128)).then_inc(c_ld[4], 16)
            sp.dma_start(vec[:, :, :], d["vec"].rearrange("a p f -> p a f")).then_inc(c_ld[5], 16)
            sp.dma_start(eb[:, :, :], d["eb"].rearrange("e p f -> p e f")).then_inc(c_ld[6], 16)

            def body(k):
                b = k.b
                if k.nxt:
                    for half in range(2):
                        if not (k.static and b < 0):
                            sp.wait_ge(e_low, 4 * (b + 1))
                        sp.dma_start(w_st[:, half, :], d["we"][one(b + 1), half, :, :].rearrange("o p n -> p (o n)")
                                     ).then_inc(w_ld[half], 16)
                    if k.prev:
                        sp.wait_ge(y_norm, 4 * b)
                    for f in range(FT):
                        sp.dma_start(yT[k.pn][:, f, :, :],
                                     halves(d["y"], k.hp + 1, k.pn, f).rearrange("a o p t -> p (a o) t")
                                     ).then_inc(y_ld[k.pn], 16)
                        if k.prev and f == 0:
                            sp.wait_ge(x4_s, 4 * b)
                        sp.dma_start(x3[k.pn][:, f, :, :],
                                     halves(d["x2"], k.hp + 1, k.pn, f).rearrange("a o p t -> p (a o) t")
                                     ).then_inc(x_ld[k.pn], 16)
                if k.prev:
                    if not k.nxt:
                        sp.wait_ge(x4_s, 4 * b)
                    for f in range(FT):
                        sp.dma_start(halves(d["out"], k.hp, k.pn, f).rearrange("a o p t -> p (a o) t"),
                                     xo[:, f, :, :]).then_inc(o_st, 16)

            run_batches(sp, table, body)
            sp.wait_ge(o_st, 32 * E8)

        @block.gpsimd
        def _(pool):
            nc.gpsimd.memset(ones[:, :], 1.0).then_inc(ones_s, 1)

            def body(k):
                b = k.b
                n = b + 1
                if k.nxt:
                    for f in range(FT):
                        pool.wait_ge(y_norm, 4 * n + (2 + f + 1))
                        nc.gpsimd.tensor_tensor(yl[:, f, :], yf[:, f, :], yh[:, f, :], ALU.subtract).then_inc(y_low, 1)
                    for f in range(FT):
                        pool.wait_ge(job_out, k.job(f"Z{f}n"))
                        if f == 0:
                            pool.wait_ge(x_ld[k.pn], 32 * (k.hp + 2))
                        v = x3[k.pn][:, f, :, :].rearrange("p a t -> p (a t)")
                        nc.gpsimd.tensor_tensor(v, v, zf[:, f, :], ALU.add).then_inc(x3_s, 1)
                if k.att:
                    for f in range(FT):
                        pool.wait_ge(w2_out, FT * b + (f + 1))
                        nc.gpsimd.tensor_tensor(y2l[:, f, :], y2f[:, f, :], y2h[:, f, :], ALU.subtract
                                                ).then_inc(y2_low, 1)
                if k.nxt:
                    for f in range(FT):
                        pool.wait_ge(job_out, k.job(f"TD{f}n"))
                        nc.gpsimd.tensor_tensor(h2l[:, f, :], h2f[:, f, :], h2h[:, f, :], ALU.subtract
                                                ).then_inc(h2_low, 1)
                    for f in range(FT):
                        pool.wait_ge(job_out, k.job(f"G{f}n"))
                        nc.gpsimd.tensor_tensor(gf[:, f, :], gf[:, f, :], hf[:, f, :], ALU.add).then_inc(g_sum, 1)
                        pool.wait_ge(g_high, FT * n + (f + 1))
                        nc.gpsimd.tensor_tensor(gl[k.pn][:, f, :], gf[:, f, :], gh[k.pn][:, f, :], ALU.subtract
                                                ).then_inc(g_low, 1)

            run_batches(pool, table, body)

        @block.scalar
        def _(act):
            nc.scalar.activation(keep["norm2"][:, :, :], keep["norm2"][:, :, :], ACT.Sqrt).then_inc(root, 1)
            act.wait_ge(gsel, 3)
            act.wait_ge(c_ld[4], 16)
            for f in range(FT):
                nc.scalar.activation(wsm[:, 0, f, :], wsm[:, 0, f, :], ACT.Copy, scale=gsc[:, f:f + 1]).then_inc(cw_sc, 1)
            act.wait_ge(cw_sc, FT)
            nc.scalar.activation(wsh[:, :, :, :], wsm[:, :, :, :], ACT.Copy, scale=WS).then_inc(cw_high, 1)

            def body(k):
                b = k.b
                n = b + 1
                for s in range(NS):
                    if k.nxt and s == 0:
                        if k.static and b < 0:
                            act.wait_ge(nsel, 3)
                        else:
                            act.wait_ge(y_low, FT * n)
                        act.wait_ge(y_ld[k.pn], 32 * (k.hp + 2))
                        for dst, nm in ((yf, 0), (yh, 1)):
                            for f in range(FT):
                                nc.scalar.activation(dst[:, f, :], yT[k.pn][:, f, :, :].rearrange("p a t -> p (a t)"),
                                                     ACT.Copy, scale=rsc[:, f:f + 1]).then_inc(y_norm, 1)
                    name = k.slot.get(s)
                    if name is not None:
                        act.wait_ge(job_done, k.job(name))
                        i = int(name[-2])
                        kind = name[:-2]
                        hv = lambda a, q: a[:, q * EH:q * EH + EH]
                        if kind == "Z":
                            if i == 0:
                                act.wait_ge(gab_s, 2 * n + 2)
                            if not (k.static and b < 0):
                                act.wait_ge(x3_s, FT * b + (i + 1))
                            for q in range(2):
                                ins = nc.scalar.activation(hv(zf[:, i, :], q), hv(X[:, :], q), ACT.Identity,
                                                           bias=gab[:, q, i:i + 1], scale=ga64[:, q, i:i + 1])
                            ins.then_inc(job_out, 1)
                        elif kind in ("TA", "TC"):
                            nc.scalar.activation(xtok[:, 2 * i:2 * i + 2, :],
                                                 X[:, :].rearrange("p (t c) -> p t c", t=2), ACT.Copy
                                                 ).then_inc(job_out, 1)
                        elif kind == "TB":
                            for q in range(2):
                                ins = nc.scalar.activation(hv(hf[:, i, :], q), hv(X[:, :], q), ACT.Identity,
                                                           bias=cur[:, q, 6 + i:7 + i], scale=cur[:, q, 8 + i:9 + i])
                            ins.then_inc(job_out, 1)
                        elif kind == "TD":
                            if not (k.static and b < 0):
                                act.wait_ge(h2_low, FT * b + (i + 1))
                            nc.scalar.activation(h2f[:, i, :], X[:, :], ACT.Identity, bias=vec[:, 1, i:i + 1],
                                                 scale=vec[:, 0, i:i + 1]).then_inc(h2_high, 1)
                            nc.scalar.activation(h2h[:, i, :], X[:, :], ACT.Identity, bias=vec[:, 1, i:i + 1],
                                                 scale=vec[:, 0, i:i + 1]).then_inc(job_out, 1)
                        elif kind == "G":
                            if not (k.static and b < 0):
                                act.wait_ge(g_low, FT * b + (i + 1))
                            nc.scalar.activation(gf[:, i, :], X[:, :], ACT.Identity, bias=vec[:, 2, i:i + 1],
                                                 scale=1 / WS).then_inc(job_out, 1)
                    if k.att and s < HM:
                        t = NA * b + s
                        if s == 0:
                            act.wait_ge(ebc, n)
                        act.wait_ge(a_done, t + 1)
                        if not (k.first and s < 2):
                            act.wait_ge(split, HM * b + (s - 1))
                        nc.scalar.activation(af[:, s % 2, :], PA[:, s % 4, :], ACT.Gelu, bias=eb_cur[:, s:s + 1],
                                             scale=1 / WS).then_inc(a_out, 1)
                    if k.nxt and 3 <= s < 7:
                        c = s - 3
                        half, o = c // 2, (c % 2) * HID
                        if c % 2 == 0:
                            act.wait_ge(w_ld[half], 16 * (n + 1))
                        nc.scalar.activation(eh[k.pn][:, half, o:o + HID], w_st[:, half, o:o + HID], ACT.Copy,
                                             scale=WS).then_inc(e_high, 1)
                    for at, q in ((NORM_AT[0] + 1, 0), (NORM_AT[1] + 1, 1)):
                        if k.nxt and s == at:
                            nth = 2 * n + (q + 1)
                            act.wait_ge(ve_s, nth)
                            nc.scalar.activation(lnr[:, 0, :], ve[:, :], ACT.Ln).then_inc(ln_s, 1)
                            act.wait_ge(ln_s, nth)
                            nc.scalar.activation(lnr[:, 1, :], lnr[:, 0, :], ACT.Exp, scale=-0.5).then_inc(guess, 1)
                    if k.att and s == 11:
                        for f in range(FT):
                            act.wait_ge(w2_done, FT * b + (f + 1))
                            sc = 1 / (WS * HS)
                            nc.scalar.activation(y2f[:, f, :], PW[:, f, :], ACT.Identity,
                                                 bias=eb_cur[:, HM + f:HM + f + 1], scale=sc).then_inc(y2_s, 1)
                            nc.scalar.activation(y2h[:, f, :], PW[:, f, :], ACT.Identity,
                                                 bias=eb_cur[:, HM + f:HM + f + 1], scale=sc).then_inc(w2_out, 1)
                    if k.att and s in (12, 13):
                        f = s - 12
                        act.wait_ge(a_done, NA * b + (HM + f + 1))
                        if k.prev and f == 0:
                            act.wait_ge(x4_s, 4 * b)
                        nc.scalar.activation(of[:, f, :], PA[:, f, :], ACT.Gelu, bias=vec[:, 3, f:f + 1],
                                             scale=1 / WS).then_inc(a_out, 1)
                if k.nxt:
                    for f in range(FT):
                        act.wait_ge(g_sum, FT * n + (f + 1))
                        nc.scalar.activation(gh[k.pn][:, f, :], gf[:, f, :], ACT.Copy).then_inc(g_high, 1)

            run_batches(act, table, body)

        @block.vector
        def _(dve):
            dve.wait_ge(root, 1)
            nc.vector.tensor_reduce(nsum[:, :].rearrange("p (g j) -> p g j", j=HG),
                                    keep["norm2"][:, :, :].rearrange("p (b g) (t j) -> p g j b t", g=NG, j=HG),
                                    mybir.AxisListType.XY, ALU.add).then_inc(nred, 1)
            dve.wait_ge(ntot, 1)
            nc.vector.tensor_scalar(rinv[:, :], X[:, 0:H], 1.0 / (B * T), 1e-5, ALU.mult, ALU.max).then_inc(ninv, 1)
            dve.wait_ge(ninv, 1)
            nc.vector.reciprocal(rinv[:, :], rinv[:, :]).then_inc(ninv, 1)
            dve.wait_ge(ninv, 2)
            dve.wait_ge(c_ld[0], 16)
            for f in range(FT):
                nc.vector.tensor_tensor(selw[:, 0, f, :], hsel[:, f, :], rinv[:, :], ALU.mult).then_inc(nsel, 1)
            dve.wait_ge(nsel, 2)
            nc.vector.tensor_reduce(rsc[:, :], selw[:, 0, :, :], AX, ALU.add).then_inc(nsel, 1)
            dve.wait_ge(c_ld[1], 16)
            nc.vector.tensor_scalar(gates[:, :], gates[:, :], 0.0, 1.0, ALU.max, ALU.min).then_inc(ninv, 1)
            dve.wait_ge(c_ld[3], 16)
            nc.vector.tensor_scalar(gcol[:, :], gcol[:, :], 0.0, 1.0, ALU.max, ALU.min).then_inc(ninv, 1)
            dve.wait_ge(ninv, 4)
            nc.vector.tensor_scalar(gates[:, :], gates[:, :], 1.0 / H, None, ALU.mult).then_inc(ninv, 1)
            nc.vector.tensor_scalar(gcol[:, :], gcol[:, :], 1.0 / H, None, ALU.mult).then_inc(ninv, 1)
            dve.wait_ge(ninv, 6)
            for f in range(FT):
                nc.vector.tensor_tensor(selw[:, 1, f, :], hsel[:, f, :], gates[:, :], ALU.mult).then_inc(gsel, 1)
            dve.wait_ge(gsel, 2)
            nc.vector.tensor_reduce(gsc[:, :], selw[:, 1, :, :], AX, ALU.add).then_inc(gsel, 1)
            dve.wait_ge(bsum, 1)
            nc.vector.tensor_copy(bob[:, :], X[:, H:H + FT]).then_inc(bob_s, 1)
            dve.wait_ge(cw_high, 1)
            nc.vector.scalar_tensor_tensor(out=wsl[:, :, :, :].rearrange("p a k n -> p (a k n)"),
                                           in0=wsm[:, :, :, :].rearrange("p a k n -> p (a k n)"), scalar=WS,
                                           in1=wsh[:, :, :, :].rearrange("p a k n -> p (a k n)"),
                                           op0=ALU.mult, op1=ALU.subtract).then_inc(cw_low, 1)
            dve.wait_ge(bob_s, 1)
            for k_ in (5, 6):
                dve.wait_ge(c_ld[k_], 16)

            def norm(k, q, stage):
                n = k.b + 1
                nth = 2 * n + q
                if stage == 0:
                    dve.wait_ge(job_out, k.job("TA1n" if q == 0 else "TC1n"))
                    for tt in range(TT):
                        nc.vector.bn_stats(st6[:, tt, :], xtok[:, tt, :]).then_inc(bns, 1)
                    dve.wait_ge(bns, nth * TT + TT)
                    nc.vector.memset(fence[:, :], 0.0)
                    for tt in range(TT):
                        nc.vector.bn_aggr(mv[:, tt, :], st6[:, tt, :]).then_inc(agg, 1)
                    dve.wait_ge(agg, nth * TT + TT)
                    nc.vector.tensor_scalar(ve[:, :], mv[:, :, 1], EPS, None, ALU.add).then_inc(ve_s, 1)
                    return
                dve.wait_ge(guess, nth + 1)
                nc.vector.tensor_tensor(lnr[:, 2, :], lnr[:, 1, :], lnr[:, 1, :], ALU.mult).then_inc(newton, 1)
                dve.wait_ge(newton, (nth + 1) * NEWTON - 2)
                nc.vector.scalar_tensor_tensor(out=lnr[:, 2, :], in0=lnr[:, 2, :], scalar=-0.5, in1=ve[:, :],
                                               op0=ALU.mult, op1=ALU.mult).then_inc(newton, 1)
                dve.wait_ge(newton, (nth + 1) * NEWTON - 1)
                nc.vector.scalar_tensor_tensor(out=rstd[:, :], in0=lnr[:, 2, :], scalar=1.5, in1=lnr[:, 1, :],
                                               op0=ALU.add, op1=ALU.mult).then_inc(newton, 1)
                dve.wait_ge(newton, (nth + 1) * NEWTON)
                for tt in range(TT):
                    nc.vector.tensor_scalar(xn[:, tt, :], xtok[:, tt, :], mv[:, tt, 0:1], rstd[:, tt:tt + 1],
                                            ALU.subtract, ALU.mult).then_inc(xn_s, 1)

            def body(k):
                b = k.b
                n = b + 1
                modq = keep["mod"][:, 1, :, :].rearrange("p (a q) c -> p a q c", a=2)
                for s in range(NS):
                    if k.nxt and s == 0:
                        nc.vector.tensor_copy(cur[:, :, :], modq[:, :, one(k.hp + 1) if not (k.static) else one((b + 1) // 2), :]
                                              .rearrange("p a q c -> p (a q) c")).then_inc(cur_s, 1)
                        dve.wait_ge(cur_s, n + 1)
                        nc.vector.tensor_scalar(ga64[:, :, :], cur[:, :, 4:6], 1 / WS, None, ALU.mult).then_inc(gab_s, 1)
                        nc.vector.tensor_tensor(gab[:, :, :], cur[:, :, 4:6],
                                                bob[:, :].unsqueeze(1).to_broadcast([128, 2, FT]), ALU.mult
                                                ).then_inc(gab_s, 1)
                    if k.att and s == 0:
                        nc.vector.tensor_copy(eb_cur[:, :].unsqueeze(1), eb[:, one(b), :]).then_inc(ebc, 1)
                        if k.prev:
                            dve.wait_ge(x4_s, 4 * b)
                            nc.vector.memset(fence[:, :], 0.0)
                        qb = (one(b // 2) if k.static else one(k.hp + 1) if k.par == 0 else one(k.hp))
                        nc.vector.tensor_copy(gcur[:, :, :], modq[:, :, qb, :].rearrange("p a q c -> p (a q) c")
                                              ).then_inc(gcur_s, 1)
                    if k.att and s < HM:
                        t = HM * b + s
                        dve.wait_ge(a_out, NA * b + (s + 1))
                        nc.vector.tensor_scalar(Hh[:, s, :], af[:, s % 2, :], HS, None, ALU.mult).then_inc(high, 1)
                        dve.wait_ge(high, t + 1)
                        nc.vector.scalar_tensor_tensor(out=Hl[:, s, :], in0=af[:, s % 2, :], scalar=HS, in1=Hh[:, s, :],
                                                       op0=ALU.mult, op1=ALU.subtract).then_inc(split, 1)
                    if k.nxt and s == NORM_AT[0]:
                        norm(k, 0, 0)
                    if k.nxt and s == NORM_AT[0] + 1:
                        norm(k, 0, 1)
                    if k.nxt and 3 <= s < 7:
                        c = s - 3
                        half, o = c // 2, (c % 2) * HID
                        dve.wait_ge(e_high, 4 * n + (c + 1))
                        nc.vector.scalar_tensor_tensor(out=el[k.pn][:, half, o:o + HID], in0=w_st[:, half, o:o + HID],
                                                       scalar=WS, in1=eh[k.pn][:, half, o:o + HID],
                                                       op0=ALU.mult, op1=ALU.subtract).then_inc(e_low, 1)
                    if k.nxt and s == NORM_AT[1]:
                        norm(k, 1, 0)
                    if k.nxt and s == NORM_AT[1] + 1:
                        norm(k, 1, 1)
                    if k.att and s in (13, 14):
                        f = s - 13
                        dve.wait_ge(a_out, NA * b + (HM + f + 1))
                        if f == 0:
                            dve.wait_ge(gcur_s, n)
                            if k.prev:
                                dve.wait_ge(o_st, 32 * b)
                        for q in range(2):
                            nc.vector.scalar_tensor_tensor(
                                out=xo[:, f, q, :], in0=of[:, f, q * EH:q * EH + EH],
                                scalar=gcur[:, q, 10 + f:11 + f], in1=x3[k.par][:, f, q, :],
                                op0=ALU.mult, op1=ALU.add).then_inc(x4_s, 1)

            run_batches(dve, table, body)

        @block.tensor
        def _(pe):
            id32 = keep["id32"]
            pe.wait_ge(ones_s, 1)
            pe.wait_ge(nred, 1)
            nc.tensor.matmul(X[:, 0:H], ones[:, :], nsum[:, :], start=True, stop=True).then_inc(ntot, 1)
            pe.wait_ge(c_ld[2], 16)
            pe.wait_ge(ninv, 6)
            for f in range(FT):
                ins = nc.tensor.matmul(X[:, H + f:H + f + 1], bo[:, f * 128:f * 128 + 128], gcol[:, :],
                                       start=True, stop=True)
            ins.then_inc(bsum, 1)
            pe.wait_ge(cw_low, 1)

            def product(out, wh_, wl_, xh, xl, kts=range(FT), start=True, stop=True):
                ops = [(a(kt), c(kt)) for kt in kts for a, c in ((wh_, xh), (wh_, xl), (wl_, xh))]
                for n_, (a, c) in enumerate(ops):
                    ins = nc.tensor.matmul(out, a, c, start=start and n_ == 0, stop=stop and n_ == len(ops) - 1)
                return ins

            def small(a, m, t):
                return lambda kt: t[:, a, kt, m * 128:m * 128 + 128]

            def body(k):
                b = k.b
                n = b + 1

                def job(name):
                    if not (k.static and k.before(name) == 0):
                        pe.wait_ge(job_out, k.before(name))
                    i, kind = int(name[-2]), name[:-2]
                    if kind == "Z":
                        pe.wait_ge(y_low, FT * n + FT)
                        ins = product(X[:, :], small(0, i, wsh), small(0, i, wsl), lambda kt: yh[:, kt, :],
                                      lambda kt: yl[:, kt, :])
                    elif kind == "G":
                        pe.wait_ge(h2_low, FT * n + FT)
                        ins = product(X[:, :], small(1, i, wsh), small(1, i, wsl), lambda kt: h2h[:, kt, :],
                                      lambda kt: h2l[:, kt, :])
                    elif kind in ("TA", "TC"):
                        if kind == "TA":
                            pe.wait_ge(x3_s, FT * n + FT)
                        for a in range(2):
                            for f in range(FT):
                                o, tt = (a * FT + f) * 128, 2 * i + a
                                if kind == "TA":
                                    src = x3[k.pn][:, f, tt // 2, (tt % 2) * 128:(tt % 2) * 128 + 128]
                                else:
                                    src = hf[:, f, tt * 128:tt * 128 + 128]
                                ins = nc.tensor.transpose(X[:, o:o + 128], src, id32[:, :])
                    else:
                        pe.wait_ge(xn_s, (2 * n + (1 if kind == "TB" else 2)) * TT)
                        for tt in range(TT):
                            ins = nc.tensor.transpose(X[:, tt * 128:tt * 128 + 128], xn[:, tt, i * 128:i * 128 + 128],
                                                      id32[:, :])
                    ins.then_inc(job_done, 1)

                for s in range(NS):
                    if s in k.slot:
                        job(k.slot[s])
                    if k.att and s < HM:
                        if s == 0:
                            pe.wait_ge(g_low, FT * n)
                            pe.wait_ge(e_low, 4 * n)
                        if s < 4 and not k.first:
                            pe.wait_ge(a_out, NA * b + (-1 if s == 0 else 0))
                        elif s >= 4:
                            pe.wait_ge(a_out, NA * b + (s - 3))
                        product(PA[:, s % 4, :], lambda kt: eh[k.par][:, 0, kt * HID + s * 128:kt * HID + s * 128 + 128],
                                lambda kt: el[k.par][:, 0, kt * HID + s * 128:kt * HID + s * 128 + 128],
                                lambda kt: gh[k.par][:, kt, :], lambda kt: gl[k.par][:, kt, :]).then_inc(a_done, 1)
                    elif k.att and s < 12:
                        c = s - HM
                        pe.wait_ge(split, HM * b + (2 * c + 2))
                        if c == 0 and not k.first:
                            pe.wait_ge(w2_out, FT * b)
                        for f in range(FT):
                            ins = product(PW[:, f, :], lambda kt: eh[k.par][:, 1, kt * C + f * 128:kt * C + f * 128 + 128],
                                          lambda kt: el[k.par][:, 1, kt * C + f * 128:kt * C + f * 128 + 128],
                                          lambda kt: Hh[:, kt, :], lambda kt: Hl[:, kt, :], range(2 * c, 2 * c + 2),
                                          c == 0, c == 3)
                            if c == 3:
                                ins.then_inc(w2_done, 1)
                    elif k.att and s in (12, 13):
                        f = s - 12
                        pe.wait_ge(y2_low, FT * n)
                        pe.wait_ge(a_out, NA * b + HM)
                        product(PA[:, f, :], small(2, f, wsh), small(2, f, wsl), lambda kt: y2h[:, kt, :],
                                lambda kt: y2l[:, kt, :]).then_inc(a_done, 1)

            run_batches(pe, table, body)


def program(nc, d):
    with ExitStack() as ctx:
        sb = lambda n, s, t=F32: ctx.enter_context(nc.sbuf_tensor(n, s, t))
        keep = {"id32": sb("id32", [128, 128]), "id16": sb("id16", [128, 128], F16),
                "mod": sb("mod", [128, 2, B, 12]),
                "norm2": sb("norm2", [128, B * NG, H])}
        dram = lambda n, s: nc.dram_tensor(n, s, F32).ap()
        x1, x2, y = dram("x1", [B, C, T]), dram("x2", [B, C, T]), dram("y", [B, C, T])
        x2_tok = dram("x2_tok", [B, T, C])
        setup(nc, d, keep)
        attention(nc, 0, {"wqkv": d["wqkv0"], "wproj": d["wproj"], "rope": d["rope"], "g_rms": d["g_rms"],
                          "x_tok": d["x_tok"], "x_feat": d["x_feat"], "x_out": x1}, keep)
        mlp0(nc, d | {"x1": x1, "x2": x2, "x2_tok": x2_tok}, keep)
        attention(nc, 1, {"wqkv": d["wqkv1"], "bqkv": d["bqkv"], "x_tok": x2_tok, "x_out": y}, keep)
        halves = lambda t: t.rearrange("(a q) c t -> a q c t", a=2)
        experts(nc, d | {"y": halves(y), "x2": halves(x2), "out": halves(d["out"])}, keep)


def kernel(**inputs):
    import ml_dtypes as _ml
    import numpy as _np
    import concourse.bacc as _bacc
    from concourse import mybir as _mybir
    from concourse.bass_utils import run_bass_kernel_spmd as _run

    a = {n: _np.asarray(v) for n, v in inputs.items()}
    f0, f1 = "L0_ffn_", "L1_ffn_"

    def rows(w):
        return w.reshape(-1, 128, w.shape[-1]).transpose(1, 0, 2).reshape(128, -1)

    def cols(v):
        return v.reshape(-1, 128).T

    def heads(w):
        return w.transpose(1, 0, 2).reshape(C, C)

    inv = 1.0 / 10000.0 ** (_np.arange(0, HD, 2, dtype=_np.float32) / HD)
    angle = _np.outer(_np.arange(T, dtype=_np.float32), inv)
    cos, sin = (f(angle).astype(_ml.bfloat16).astype(_np.float32) for f in (_np.cos, _np.sin))
    rope = _np.stack([_np.concatenate([cos, cos], 1), _np.concatenate([sin, -sin], 1)], 1)
    head_of = (_np.arange(C)[:, None] // HD == _np.arange(H)[None, :]).astype(_np.float32)

    x = a["L0_attn_x"]
    w_ffn0 = _np.concatenate([rows(a[f0 + n].T) for n in ("w1_w", "w2_w", "h1_w", "h2_w", "w3_w")], 1)
    data = {
        "c": _np.stack([a["L0_c"].T, a["L1_c"].T]),
        "wmod": _np.stack([a["L0_wmod"], a["L1_wmod"]]),
        "wqkv0": _np.concatenate([a["L0_attn_w" + n].T for n in "qkv"], 1),
        "wproj": a["L0_attn_wproj"].T,
        "rope": rope,
        "g_rms": a["L0_attn_g_rms"],
        "x_tok": x,
        "x_feat": x.transpose(0, 2, 1),
        "w_ffn0": w_ffn0.reshape(128, -1, 2 * HID).transpose(1, 0, 2),
        "s_ffn0": _np.concatenate([cols(a[f0 + n]) for n in ("w1_s", "w2_s", "h1_s", "h2_s", "w3_s")], 1),
        "wqkv1": _np.concatenate([heads(a["L1_attn_W" + n]) for n in "qkv"], 1),
        "bqkv": _np.concatenate([a["L1_attn_b" + n].reshape(-1) for n in "qkv"]),
        "head_of": head_of.reshape(FT, 128, H).transpose(1, 0, 2),
        "gate": a["L1_attn_gate"],
        "bo": a["L1_attn_bo"],
        "w_small": _np.stack([a["L1_attn_Wo"].reshape(C, C), a[f1 + "attn_w"], a[f1 + "next_w"]]),
        "vec": _np.stack([cols(a[f1 + n]) for n in ("ln_g", "ln_b", "attn_b", "next_b")]),
        "eb": _np.stack([_np.concatenate([cols(a[f1 + "b1"][e]), cols(a[f1 + "b2"][e])], 1) for e in range(E8)]),
        "we": _np.stack([_np.stack([rows(a[f1 + "w1"][e]), rows(a[f1 + "w2"][e])]) for e in range(E8)]),
    }
    nc = _bacc.Bacc("TRN2", target_bir_lowering=False, num_devices=1)
    arrays, d = {}, {}
    for name, v in data.items():
        v = _np.ascontiguousarray(v)
        arrays[f"in_{name}_dram"] = v
        d[name] = nc.dram_tensor(f"in_{name}_dram", v.shape, _mybir.dt.from_np(v.dtype), kind="ExternalInput").ap()
    d["out"] = nc.dram_tensor("out_dram", (B, C, T), F32, kind="ExternalOutput").ap()
    program(nc, d)
    r = _run(nc, [arrays], core_ids=[0])
    return _np.ascontiguousarray(r.results[0]["out_dram"].transpose(0, 2, 1))
```
